# Optimizing a Trainium2 kernel written in Bass

```python
import numpy as np
import jax
import jax.numpy as jnp

def _softmax(x, axis=-1):
    return jax.nn.softmax(x, axis=axis)

def _gelu(x):
    return jax.nn.gelu(x, approximate=True)

def _silu(x):
    return jax.nn.silu(x)

def _sigmoid(x):
    return jax.nn.sigmoid(x)

def _layernorm(x, axis=-1, eps=1e-05):
    m = jnp.mean(x, axis=axis, keepdims=True)
    v = jnp.var(x, axis=axis, keepdims=True)
    return (x - m) / jnp.sqrt(v + eps)

def _scatter_add(tgt, idx, src, axis=0):
    return tgt.at[idx].add(src)

def _segment_sum(src, seg, n):
    return jax.ops.segment_sum(src, seg, n)
kernel_name = 'mk_sandwich_d1_jaxref_r8_333c8b'

def setup_inputs(seed: int=0):
    np.random.seed(seed)
    _w = jnp.asarray

    def _L0_attn_setup():
        import jax, jax.numpy as jnp
        import numpy as np
        B, N, HID = (1, 256, 512)
        H, KVH, D, W = (32, 8, 128, 64)
        THETA = 10000.0
        GATE_NORM = 16.0

        def rope(x, pos):
            half = jnp.arange(D // 2, dtype=jnp.float32)
            inv = 1.0 / THETA ** (2.0 * half / D)
            fr = pos[:, None].astype(jnp.float32) * inv[None, :]
            emb = jnp.concatenate([fr, fr], axis=-1)
            cos, sin = (jnp.cos(emb)[None, None], jnp.sin(emb)[None, None])
            x1, x2 = jnp.split(x, 2, axis=-1)
            rot = jnp.concatenate([-x2, x1], axis=-1)
            return x * cos + rot * sin

        def gla_scan(q, k, v, g):
            qt, kt, vt, gt = (jnp.moveaxis(t, 2, 0) for t in (q, k, v, g))
            b, h = (q.shape[0], q.shape[1])
            S0 = jnp.zeros((b, h, D, D), jnp.float32)

            def step(S, x):
                q_t, k_t, v_t, g_t = x
                S = S * jnp.exp(g_t)[..., None] + k_t[..., None] * v_t[..., None, :]
                return (S, jnp.einsum('bhk,bhkv->bhv', q_t, S))
            _, o = jax.lax.scan(step, S0, (qt, kt, vt, gt))
            return jnp.moveaxis(o, 0, 2)

        def sliding_window_attn(q, k, v):
            b, h, n, d = q.shape
            nb = n // W
            qb = q.reshape(b, h, nb, W, d)

            def two_blocks(x):
                xb = x.reshape(b, h, nb, W, d)
                prev = jnp.concatenate([jnp.zeros_like(xb[:, :, :1]), xb[:, :, :-1]], axis=2)
                return jnp.concatenate([prev, xb], axis=3)
            kb, vb = (two_blocks(k), two_blocks(v))
            scores = jnp.einsum('bhnqd,bhnkd->bhnqk', qb, kb) / jnp.sqrt(jnp.float32(d))
            a = jnp.arange(W)[:, None]
            c = jnp.arange(2 * W)[None, :]
            rel = a + W - c
            base = (rel >= 0) & (rel <= W)
            blk = jnp.arange(nb)[:, None, None]
            keypos = (blk - 1) * W + c[None]
            mask = base[None] & (keypos >= 0)
            scores = jnp.where(mask[None, None], scores, -jnp.inf)
            p = jax.nn.softmax(scores, axis=-1)
            ob = jnp.einsum('bhnqk,bhnkd->bhnqd', p, vb)
            return ob.reshape(b, h, n, d)
        key = jax.random.key(seed)
        ks = jax.random.split(key, 5)
        s = 0.02
        return {'hidden_states': jax.random.normal(ks[0], (B, N, HID), jnp.float32), 'Wq': jax.random.normal(ks[1], (HID, H * D), jnp.float32) * s, 'Wk': jax.random.normal(ks[2], (HID, KVH * D), jnp.float32) * s, 'Wv': jax.random.normal(ks[3], (HID, KVH * D), jnp.float32) * s, 'Wo': jax.random.normal(ks[4], (H * D, HID), jnp.float32) * s}
    _L0_attn_in = _L0_attn_setup()

    def _L0_ffn_setup():
        import jax, jax.numpy as jnp
        import numpy as np
        NF4_CODE = jnp.array([-1.0, -0.6961928009986877, -0.5250730514526367, -0.39491748809814453, -0.28444138169288635, -0.18477343022823334, -0.09105003625154495, 0.0, 0.07958029955625534, 0.16093020141124725, 0.24611230194568634, 0.33791524171829224, 0.44070982933044434, 0.5626170039176941, 0.7229568362236023, 1.0], dtype=jnp.float32)
        BLOCKSIZE = 64

        def nf4_quant_dequant(w):
            shape = w.shape
            flat = w.reshape(-1, BLOCKSIZE)
            absmax = jnp.max(jnp.abs(flat), axis=1, keepdims=True)
            normalized = flat / jnp.where(absmax == 0, 1.0, absmax)
            bounds = (NF4_CODE[:-1] + NF4_CODE[1:]) * 0.5
            idx = jnp.searchsorted(bounds, normalized)
            return (NF4_CODE[idx] * absmax).reshape(shape)
        key = jax.random.key(seed)
        k1, k2, k3, kx = jax.random.split(key, 4)
        D, H = (512, 1376)
        scale = 0.02
        w1 = jax.random.normal(k1, (H, D), jnp.float32) * scale
        w2 = jax.random.normal(k2, (H, D), jnp.float32) * scale
        w3 = jax.random.normal(k3, (D, H), jnp.float32) * scale
        x = jax.random.normal(kx, (2, 256, D), jnp.float32)
        return {'x': x, 'w1': w1, 'w2': w2, 'w3': w3}
    _L0_ffn_in = _L0_ffn_setup()
    _d = {'L0_attn_hidden_states': _L0_attn_in['hidden_states'], 'L0_attn_Wq': _L0_attn_in['Wq'], 'L0_attn_Wk': _L0_attn_in['Wk'], 'L0_attn_Wv': _L0_attn_in['Wv'], 'L0_attn_Wo': _L0_attn_in['Wo'], 'L0_ffn_w1': _L0_ffn_in['w1'], 'L0_ffn_w2': _L0_ffn_in['w2'], 'L0_ffn_w3': _L0_ffn_in['w3']}
    _x0 = _d['L0_attn_hidden_states']
    _d['L0_attn_hidden_states'] = jax.random.normal(jax.random.fold_in(jax.random.key(seed), 1), (2, 1024, 512), dtype=_x0.dtype)
    del _x0
    return _d

def reference(L0_attn_hidden_states, L0_attn_Wq, L0_attn_Wk, L0_attn_Wv, L0_attn_Wo, L0_ffn_w1, L0_ffn_w2, L0_ffn_w3):

    def _L0_attn_ref(hidden_states, Wq, Wk, Wv, Wo):
        import jax, jax.numpy as jnp
        import numpy as np
        B, N, HID = (1, 256, 512)
        H, KVH, D, W = (32, 8, 128, 64)
        THETA = 10000.0
        GATE_NORM = 16.0

        def rope(x, pos):
            half = jnp.arange(D // 2, dtype=jnp.float32)
            inv = 1.0 / THETA ** (2.0 * half / D)
            fr = pos[:, None].astype(jnp.float32) * inv[None, :]
            emb = jnp.concatenate([fr, fr], axis=-1)
            cos, sin = (jnp.cos(emb)[None, None], jnp.sin(emb)[None, None])
            x1, x2 = jnp.split(x, 2, axis=-1)
            rot = jnp.concatenate([-x2, x1], axis=-1)
            return x * cos + rot * sin

        def gla_scan(q, k, v, g):
            qt, kt, vt, gt = (jnp.moveaxis(t, 2, 0) for t in (q, k, v, g))
            b, h = (q.shape[0], q.shape[1])
            S0 = jnp.zeros((b, h, D, D), jnp.float32)

            def step(S, x):
                q_t, k_t, v_t, g_t = x
                S = S * jnp.exp(g_t)[..., None] + k_t[..., None] * v_t[..., None, :]
                return (S, jnp.einsum('bhk,bhkv->bhv', q_t, S))
            _, o = jax.lax.scan(step, S0, (qt, kt, vt, gt))
            return jnp.moveaxis(o, 0, 2)

        def sliding_window_attn(q, k, v):
            b, h, n, d = q.shape
            nb = n // W
            qb = q.reshape(b, h, nb, W, d)

            def two_blocks(x):
                xb = x.reshape(b, h, nb, W, d)
                prev = jnp.concatenate([jnp.zeros_like(xb[:, :, :1]), xb[:, :, :-1]], axis=2)
                return jnp.concatenate([prev, xb], axis=3)
            kb, vb = (two_blocks(k), two_blocks(v))
            scores = jnp.einsum('bhnqd,bhnkd->bhnqk', qb, kb) / jnp.sqrt(jnp.float32(d))
            a = jnp.arange(W)[:, None]
            c = jnp.arange(2 * W)[None, :]
            rel = a + W - c
            base = (rel >= 0) & (rel <= W)
            blk = jnp.arange(nb)[:, None, None]
            keypos = (blk - 1) * W + c[None]
            mask = base[None] & (keypos >= 0)
            scores = jnp.where(mask[None, None], scores, -jnp.inf)
            p = jax.nn.softmax(scores, axis=-1)
            ob = jnp.einsum('bhnqk,bhnkd->bhnqd', p, vb)
            return ob.reshape(b, h, n, d)
        b, n, _ = hidden_states.shape
        grp = H // KVH
        q = hidden_states @ Wq
        k = hidden_states @ Wk
        v = hidden_states @ Wv
        g = k
        q = q.reshape(b, n, H, D).transpose(0, 2, 1, 3)
        k = k.reshape(b, n, KVH, D).transpose(0, 2, 1, 3)
        v = v.reshape(b, n, KVH, D).transpose(0, 2, 1, 3)
        g = g.reshape(b, n, KVH, D).transpose(0, 2, 1, 3)
        k = jnp.repeat(k, grp, axis=1)
        v = jnp.repeat(v, grp, axis=1)
        g = jnp.repeat(g, grp, axis=1)
        sq, sk, sv = (q, k, v)
        qs = jax.nn.softmax(q.astype(jnp.float32), axis=-1)
        ks_ = jax.nn.softmax(k.astype(jnp.float32), axis=-1)
        gs = jax.nn.log_sigmoid(g.astype(jnp.float32)) / GATE_NORM
        o_lin = gla_scan(qs, ks_, v.astype(jnp.float32), gs)
        pos = jnp.arange(n)
        sq = rope(sq, pos)
        sk = rope(sk, pos)
        y = sliding_window_attn(sq, sk, sv)
        o_ = 0.5 * y + 0.5 * o_lin
        o_ = o_.astype(jnp.bfloat16).astype(jnp.float32)
        o = o_.transpose(0, 2, 1, 3).reshape(b, n, H * D) @ Wo
        return o

    def _L0_ffn_ref(x, w1, w2, w3):
        import jax, jax.numpy as jnp
        import numpy as np
        NF4_CODE = jnp.array([-1.0, -0.6961928009986877, -0.5250730514526367, -0.39491748809814453, -0.28444138169288635, -0.18477343022823334, -0.09105003625154495, 0.0, 0.07958029955625534, 0.16093020141124725, 0.24611230194568634, 0.33791524171829224, 0.44070982933044434, 0.5626170039176941, 0.7229568362236023, 1.0], dtype=jnp.float32)
        BLOCKSIZE = 64

        def nf4_quant_dequant(w):
            shape = w.shape
            flat = w.reshape(-1, BLOCKSIZE)
            absmax = jnp.max(jnp.abs(flat), axis=1, keepdims=True)
            normalized = flat / jnp.where(absmax == 0, 1.0, absmax)
            bounds = (NF4_CODE[:-1] + NF4_CODE[1:]) * 0.5
            idx = jnp.searchsorted(bounds, normalized)
            return (NF4_CODE[idx] * absmax).reshape(shape)
        dq1 = nf4_quant_dequant(w1)
        dq2 = nf4_quant_dequant(w2)
        dq3 = nf4_quant_dequant(w3)
        gate = jnp.einsum('bsd,hd->bsh', x, dq1)
        up = jnp.einsum('bsd,hd->bsh', x, dq2)
        h = jax.nn.silu(gate) * up
        return jnp.einsum('bsh,dh->bsd', h, dq3)
    x = L0_attn_hidden_states
    x = x + _layernorm(_L0_attn_ref(_layernorm(x, axis=-1), L0_attn_Wq, L0_attn_Wk, L0_attn_Wv, L0_attn_Wo), axis=-1)
    x = x + _layernorm(_L0_ffn_ref(_layernorm(x, axis=-1), L0_ffn_w1, L0_ffn_w2, L0_ffn_w3), axis=-1)
    return x

_drawn_inputs = setup_inputs


def setup_inputs(seed=0):
    import zlib

    import numpy as np

    out = dict(_drawn_inputs(seed))
    spreads = {}
    factors = {}
    for name, (base, spread) in spreads.items():
        noise = np.random.default_rng([zlib.crc32(name.encode()), seed]).standard_normal(out[name].shape)
        drawn = base * np.exp(spread * noise) if base else spread * noise
        out[name] = jnp.asarray(drawn.astype(out[name].dtype))
    for name, factor in factors.items():
        out[name] = (out[name] * factor).astype(out[name].dtype)
    return out
```

```python
from contextlib import ExitStack

import numpy as np
import concourse.bass as bass
from concourse import mybir

F32 = mybir.dt.float32
F16 = mybir.dt.float16
BF16 = mybir.dt.bfloat16
ALU = mybir.AluOpType
ACT = mybir.ActivationFunctionType
AX = mybir.AxisListType

P = 128
HID = 512
NC = HID // P
HEADS, KVH = 32, 8
GRP = HEADS // KVH
BATCH, SEQ, WIN = 2, 1024, 64
TILES = BATCH * SEQ // P
TPB = SEQ // P
STEP = 4
TURNS = KVH * TILES
STEPS = TURNS // STEP
FFN = 1376
FC = (FFN + P - 1) // P
FLAST = FFN - (FC - 1) * P
QW = GRP * P
KVW = 2 * P
WW = QW + KVW + HID
WSCALE = 256.0
HSCALE = 16.0
ATT_SCALE = float(P) ** -0.5
EPS = 1e-5
MASKED = -1e30
BLK = 64
NF4_COLS = 3 * FFN * HID // P
NF4_PIECE = 512
NF4_REST = NF4_COLS - STEPS * NF4_PIECE
NF4_STEPS = (range(0, 2), range(2, 6), range(6, 11), range(11, 15))
CODE = np.array([-1.0, -0.6961928009986877, -0.5250730514526367, -0.39491748809814453,
                 -0.28444138169288635, -0.18477343022823334, -0.09105003625154495, 0.0,
                 0.07958029955625534, 0.16093020141124725, 0.24611230194568634, 0.33791524171829224,
                 0.44070982933044434, 0.5626170039176941, 0.7229568362236023, 1.0], np.float32)
BOUND = ((CODE[:-1] + CODE[1:]) * np.float32(0.5)).astype(np.float32)
DELTA = (CODE[1:] - CODE[:-1]).astype(np.float32)


class Tile:

    def __init__(self, i, p):
        self.i, self.p = i, p

    def real(self):
        return not isinstance(self.i, int) or 0 <= STEP * self.i + self.p < TURNS

    def back(self, lag):
        q = self.p - lag
        return Tile(self.i + q // STEP, q % STEP) if q // STEP else Tile(self.i, q)

    def count(self):
        return self.i * STEP + (self.p + 1)


def wait_tile(eng, sem, t, back=0):
    v = t.count() - back
    if isinstance(v, int) and v <= 0:
        return
    eng.wait_ge(sem, v)


def turns(eng, last_lag, turn):
    for p in range(STEP):
        turn(Tile(0, p))
    with eng.Fori(1, STEPS) as i:
        for p in range(STEP):
            turn(Tile(i, p))
    for p in range(last_lag):
        turn(Tile(STEPS, p))


def norm_tiles(block, nc, src, stats, xn, xh, xl, ident, tp, s, ready):
    st, mv, sd, rs = stats
    s_st, s_mv, s_var, s_sd, s_rs, s_xn, s_tp, s_hi, s_lo = s

    @block.vector
    def _(dve):
        for t in range(TILES):
            dve.wait_ge(*ready(t))
            nc.vector.bn_stats(st[:, t, :], src[:, t, :]).then_inc(s_st, 1)
        for t in range(TILES):
            dve.wait_ge(s_st, t + 1)
            nc.vector.bn_aggr(mv[:, t, :], st[:, t, :]).then_inc(s_mv, 1)
        dve.wait_ge(s_mv, TILES)
        nc.vector.tensor_scalar(sd[:, :], mv[:, :, 1], EPS, None, ALU.add).then_inc(s_var, 1)
        dve.wait_ge(s_sd, 1)
        nc.vector.reciprocal(rs[:, :], sd[:, :]).then_inc(s_rs, 1)
        dve.wait_ge(s_rs, 1)
        for t in range(TILES + 1):
            if t < TILES:
                if t >= 2:
                    dve.wait_ge(s_tp, t - 1)
                nc.vector.tensor_scalar(xn[:, t % 2, :], src[:, t, :], mv[:, t, 0:1], rs[:, t:t + 1],
                                        ALU.subtract, ALU.mult).then_inc(s_xn, 1)
            if t >= 1:
                dve.wait_ge(s_hi, t)
                nc.vector.tensor_tensor(xl[:, :, t - 1, :], tp[(t - 1) % 2][:].rearrange("p (c n) -> p c n", c=NC),
                                        xh[:, :, t - 1, :], ALU.subtract).then_inc(s_lo, 1)

    @block.tensor
    def _(pe):
        for t in range(TILES):
            pe.wait_ge(s_xn, t + 1)
            if t >= 2:
                pe.wait_ge(s_lo, t - 1)
            for c in range(NC):
                last = nc.tensor.transpose(tp[t % 2][:, c * P:(c + 1) * P], xn[:, t % 2, c * P:(c + 1) * P], ident[:])
            last.then_inc(s_tp, 1)

    @block.scalar
    def _(act):
        act.wait_ge(s_var, 1)
        nc.scalar.activation(sd[:, :], sd[:, :], ACT.Sqrt).then_inc(s_sd, 1)
        for t in range(TILES):
            act.wait_ge(s_tp, t + 1)
            nc.scalar.activation(xh[:, :, t, :], tp[t % 2][:].rearrange("p (c n) -> p c n", c=NC),
                                 ACT.Copy).then_inc(s_hi, 1)


def layer(nc, x, wq, wk, wv, wo, wf, cosc, sinc, winmask, causal, cumsum, identc, keepc, dq, out):
    x_rows = x.rearrange("b (t p) d -> p (b t) d", p=P)
    out_rows = out.rearrange("b (t p) d -> p (b t) d", p=P)
    wq_v = wq.rearrange("(c p) (k n) -> c k p n", p=P, n=QW)
    wk_v = wk.rearrange("(c p) (k n) -> c k p n", p=P, n=P)
    wv_v = wv.rearrange("(c p) (k n) -> c k p n", p=P, n=P)
    wo_v = wo.rearrange("(k c p) n -> c k p n", p=P, c=GRP)
    wf_v = wf.rearrange("(p n) -> p n", p=P)
    dq_v = dq.rearrange("(p n) -> p n", p=P)
    wf_p = wf_v[:, 0:STEPS * NF4_PIECE].rearrange("p (i n) -> p i n", n=NF4_PIECE)
    dq_p = dq_v[:, 0:STEPS * NF4_PIECE].rearrange("p (i n) -> p i n", n=NF4_PIECE)

    with ExitStack() as whole:
        def sbw(name, shape, dt):
            return whole.enter_context(nc.sbuf_tensor(name, shape, dt))

        def sem(name):
            return whole.enter_context(nc.semaphore(name))

        xh = sbw("xh", [P, NC, TILES, P], F16)
        xl = sbw("xl", [P, NC, TILES, P], F16)
        rows = sbw("rows", [P, TILES, HID], F32)
        ident = sbw("ident", [P, P], F32)
        bank = [whole.enter_context(nc.psum_tensor(f"bank{j}", [P, 512], F32)) for j in range(8)]
        st = sbw("st", [P, TILES, 6], F32)
        mv = sbw("mv", [P, TILES, 2], F32)
        sd = sbw("sd", [P, TILES], F32)
        rs = sbw("rs", [P, TILES], F32)

        with ExitStack() as ctx:
            xn = ctx.enter_context(nc.sbuf_tensor("xn", [P, 2, HID], F32))
            x_in = [sem(f"x_in{j}") for j in range(TILES // STEP)]
            id_in = sem("id_in")
            s1 = [sem("ln1_" + n) for n in ("st", "mv", "var", "sd", "rs", "xn", "tp", "hi", "lo")]
            block = ctx.enter_context(nc.Block())

            @block.sync
            def _(sp):
                sp.dma_start(ident[:], identc).then_inc(id_in, 16)
                for j in range(TILES // STEP):
                    g = slice(j * STEP, (j + 1) * STEP)
                    sp.dma_start(rows[:, g, :], x_rows[:, g, :]).then_inc(x_in[j], 16)
                sp.wait_ge(id_in, 16)

            norm_tiles(block, nc, rows, (st, mv, sd, rs), xn, xh, xl, ident, bank, s1, lambda t: (x_in[t // STEP], 16))

        attention(nc, whole, sem, bank, rows, xh, xl, ident, wq_v, wk_v, wv_v, wo_v, wf_v, wf_p, dq_v, dq_p,
                  cosc, sinc, winmask, causal, cumsum, keepc)
        ffn(nc, sem, bank, rows, xh, xl, ident, st, mv, sd, rs, x_rows, out_rows, dq)


def attention(nc, whole, sem, bank, acc, xh, xl, ident, wq_v, wk_v, wv_v, wo_v, wf_v, wf_p, dq_v, dq_p,
              cosc, sinc, winmask, causal, cumsum, keepc):
    with ExitStack() as ctx:
        def sb(name, shape, dt=F32):
            return ctx.enter_context(nc.sbuf_tensor(name, shape, dt))

        cos = sb("cos", [P, 2, STEP, P // 2])
        sin = sb("sin", [P, 2, STEP, 2, P // 2])
        win = sb("win", [P, 2, 512], BF16)
        identb = sb("identb", [P, P], BF16)
        cau = sb("cau", [P, 512])
        cum = sb("cum", [P, 130])
        keep = sb("keep", [P, 2])
        raw_qkv = sb("raw_qkv", [P, QW + KVW])
        raw_o = sb("raw_o", [P, HID])
        wh = sb("wh", [P, 8, WW], F16)
        wl = sb("wl", [P, 8, WW], F16)
        qc = sb("qc", [P, 2, 512])
        qs = sb("qs", [P, 2, 512])
        qe = sb("qe", [P, 2, 512])
        qrT = sb("qrT", [P, 2, 2, GRP, WIN])
        qtT = sb("qtT", [P, 2, GRP, 2, WIN])
        pr = sb("pr", [P, 2, 512])
        am = sb("am", [P, 512])
        pa = sb("pa", [P, 2, 512])
        oT = sb("oT", [P, 2, GRP, 2, WIN], BF16)
        kc = sb("kc", [P, 2, P])
        ks = sb("ks", [P, 2, P])
        kabs = sb("kabs", [P, 2, P])
        kneg = sb("kneg", [P, 2, P])
        ke = sb("ke", [P, 2, P])
        ked = sb("ked", [P, 2, P])
        edT = sb("edT", [P, 2, 130])
        kt = sb("kt", [P, 2, P])
        ktT = sb("ktT", [P, 2, P])
        krT = sb("krT", [P, 4, WIN])
        va = sb("va", [P, 4, P])
        vm = sb("vm", [P, 4, P])
        sr = sb("sr", [P, 2, P])
        su = sb("su", [P, P])
        em = sb("em", [P, 2, 1])
        kmx = sb("kmx", [P, 2, 1])
        nkm = sb("nkm", [P, 2, 1])
        ksum = sb("ksum", [P, 2, 1])
        rks = sb("rks", [P, 2, 1])
        qmx = sb("qmx", [P, 2, GRP])
        nqm = sb("nqm", [P, 2, GRP])
        qsum = sb("qsum", [P, 2, GRP])
        rq = sb("rq", [P, 2, GRP])
        pmx = sb("pmx", [P, 2, GRP])
        npm = sb("npm", [P, 2, GRP])
        psm = sb("psm", [P, 2, GRP])
        rp = sb("rp", [P, 2, GRP])
        f_raw = sb("f_raw", [P, NF4_PIECE])
        f_abs = sb("f_abs", [P, NF4_PIECE])
        f_nrm = sb("f_nrm", [P, NF4_PIECE])
        f_max = sb("f_max", [P, 2, NF4_PIECE // BLK])
        f_safe = sb("f_safe", [P, NF4_PIECE // BLK])
        f_rec = sb("f_rec", [P, NF4_PIECE // BLK])
        f_s = sb("f_s", [P, 8, NF4_PIECE])
        f_acc = sb("f_acc", [P, NF4_PIECE])
        f_dq = sb("f_dq", [P, NF4_PIECE])

        PQ, PKV, X0, X1, SC, SM, PO, PW = bank
        names = """q_done kv_done small_done qrT_done at_done sc_done pt_done u_done qsT_done ktT_done o_done
            wo_done v_ev ke_ev e1_ev l1_ev q_exp dec_ev krT_ev qrT_ev p_exp ktT_ev oT_ev
            kmx_d nkm_d kabs_ev kneg_d krope_d g_d rks_d kt_d qmx_d nqm_d qrope_d rq_d qt_d pmx_d npm_d
            rp_d am_d pa_d su_d em_d sr_d acc_d qrope_p krope_p qn_p pn_p
            wqk_sc wqk_hi wqk_lo wo_sc wo_hi wo_lo raw_a raw_b consts z_id
            f_in f_absd f_maxd f_safed f_recd f_nrmd f_sd f_ad f_dqd f_out f_rin f_rest f_rout""".split()
        s = {n: sem("s_" + n) for n in names}
        part_columns = ((0, 256), (256, 512), (512, 768), (QW + KVW, WW))

        def part_of(job, part):
            lo, hi = part_columns[part]
            src = raw_qkv[:, lo:hi] if part < 3 else raw_o[:]
            kind, n = ("wqk", job * 3 + (part + 1)) if part < 3 else ("wo", job + 1)
            return src, lo, hi, s[kind + "_sc"], s[kind + "_hi"], s[kind + "_lo"], n

        t_index = lambda t: t.i % (TILES // STEP)
        block = ctx.enter_context(nc.Block())

        @block.sync
        def _(sp):
            for dst, src in ((cos[:], cosc), (sin[:], sinc), (f_s[:, 0:2, :], winmask), (cau[:], causal), (cum[:], cumsum),
                             (keep[:], keepc)):
                sp.dma_start(dst, src).then_inc(s["consts"], 16)

            def load_weights(c, k, job):
                if not (isinstance(job, int) and job == 0):
                    sp.wait_ge(s["wqk_lo"], job * 3)
                sp.dma_start(raw_qkv[:, 0:QW], wq_v[c, k]).then_inc(s["raw_a"], 16)
                sp.dma_start(raw_qkv[:, QW:QW + P], wk_v[c, k]).then_inc(s["raw_a"], 16)
                sp.dma_start(raw_qkv[:, QW + P:], wv_v[c, k]).then_inc(s["raw_a"], 16)
                if not (isinstance(job, int) and job == 0):
                    sp.wait_ge(s["wo_lo"], job)
                sp.dma_start(raw_o[:], wo_v[c, k]).then_inc(s["raw_b"], 16)

            def load_piece(i, n):
                if not (isinstance(i, int) and i == 0):
                    sp.wait_ge(s["f_nrmd"], n)
                sp.dma_start(f_raw[:], wf_p[:, i, :]).then_inc(s["f_in"], 16)

            def store_piece(i):
                sp.wait_ge(s["f_dqd"], i + 1)
                sp.dma_start(dq_p[:, i, :], f_dq[:]).then_inc(s["f_out"], 16)

            sp.dma_start(f_dq[:, 0:NF4_REST], wf_v[:, STEPS * NF4_PIECE:]).then_inc(s["f_rin"], 16)
            load_weights(0, 0, 0)
            sp.wait_ge(s["f_rest"], 5 + 29 + 1)
            sp.dma_start(dq_v[:, STEPS * NF4_PIECE:], f_dq[:, 0:NF4_REST]).then_inc(s["f_rout"], 16)
            for c in range(1, NC):
                load_weights(c, 0, c)
            load_piece(0, 0)
            for c in range(NC):
                load_weights(c, 1, NC + c)
                load_piece(c + 1, c + 1)
                if c:
                    store_piece(c - 1)
            with sp.Fori(1, KVH) as k:
                for c in range(NC):
                    load_weights(c, (k + 1) % KVH, k * NC + (NC + c))
                    load_piece((k * NC + (c + 1)) % STEPS, k * NC + (c + 1))
                    store_piece(k * NC + (c - 1))
            store_piece(STEPS - 1)
            sp.wait_ge(s["f_out"], 16 * STEPS)
            sp.wait_ge(s["f_rout"], 16)

        @block.gpsimd
        def _(pool):
            nc.gpsimd.memset(acc[:], 0.0).then_inc(s["z_id"], 1)
            nc.gpsimd.memset(vm[:], 0.0).then_inc(s["z_id"], 1)

            def rotate_q(t):
                r = t.p % 2
                wait_tile(pool, s["qrope_d"], t)
                nc.gpsimd.tensor_tensor(qc[:, r, :], qc[:, r, :], qs[:, r, :], ALU.add).then_inc(s["qrope_p"], 1)

            def rotate_k(t):
                r = t.p % 2
                wait_tile(pool, s["krope_d"], t)
                nc.gpsimd.tensor_tensor(kc[:, r, :], kc[:, r, :], ks[:, r, :], ALU.add).then_inc(s["krope_p"], 1)

            def softmax_q(t):
                r = t.p % 2
                wait_tile(pool, s["rq_d"], t)
                v = qe[:, r, :].rearrange("p (h n) -> p h n", h=GRP)
                nc.gpsimd.tensor_tensor(v, v, rq[:, r, :].unsqueeze(2).to_broadcast([P, GRP, P]),
                                        ALU.mult).then_inc(s["qn_p"], 1)

            def softmax_p(t):
                r = t.p % 2
                wait_tile(pool, s["rp_d"], t)
                v = pr[:, r, :].rearrange("p (h n) -> p h n", h=GRP)
                nc.gpsimd.tensor_tensor(v, v, rp[:, r, :].unsqueeze(2).to_broadcast([P, GRP, P]),
                                        ALU.mult).then_inc(s["pn_p"], 1)

            def split_low(job, part):
                src, lo, hi, _, high, low, n = part_of(job, part)
                pool.wait_ge(high, n)
                nc.gpsimd.tensor_tensor(wl[:, job % 8, lo:hi], src, wh[:, job % 8, lo:hi], ALU.subtract).then_inc(low, 1)

            def nf4_add(t):
                for k in NF4_STEPS[t.p]:
                    pool.wait_ge(s["f_sd"], t.i * 15 + (k + 1))
                    if k == 1:
                        if not (isinstance(t.i, int) and t.i == 0):
                            pool.wait_ge(s["f_dqd"], t.i)
                        nc.gpsimd.tensor_tensor(f_acc[:], f_s[:, 0, :], f_s[:, 1, :], ALU.add).then_inc(s["f_ad"], 1)
                    elif k > 1:
                        pool.wait_ge(s["f_ad"], t.i * 14 + (k - 1))
                        nc.gpsimd.tensor_tensor(f_acc[:], f_acc[:], f_s[:, k % 8, :], ALU.add).then_inc(s["f_ad"], 1)

            for job in range(NC):
                for part in range(4):
                    split_low(job, part)

            def turn(t):
                l1 = t.back(1)
                if l1.real():
                    rotate_q(l1)
                if t.real():
                    rotate_k(t)
                if l1.real():
                    softmax_q(l1)
                    nf4_add(l1)
                    softmax_p(l1)
                if t.real():
                    split_low(t.i + NC, t.p)

            turns(pool, 1, turn)

        @block.scalar
        def _(act):
            def k_exps(t):
                r = t.p % 2
                wait_tile(act, s["kv_done"], t)
                wait_tile(act, s["krope_d"], t)
                wait_tile(act, s["o_done"], t, 3)
                nc.scalar.activation(va[:, t.p, :], PKV[:, P:2 * P], ACT.Copy, scale=0.5 / WSCALE)
                nc.scalar.activation(vm[0:WIN, t.p, :], PKV[0:WIN, P:2 * P], ACT.Copy, scale=0.5 / WSCALE)
                nc.scalar.activation(vm[WIN:P, (t.p + 1) % 4, :], PKV[WIN:P, P:2 * P], ACT.Copy, scale=0.5 / WSCALE)\
                    .then_inc(s["v_ev"], 1)
                wait_tile(act, s["nkm_d"], t)
                nc.scalar.activation(ke[:, r, :], PKV[:, 0:P], ACT.Exp, bias=nkm[:, r, :], scale=1.0 / WSCALE,
                                     accum_out=ksum[:, r, :]).then_inc(s["ke_ev"], 1)
                nc.scalar.activation(kabs[:, r, :], PKV[:, 0:P], ACT.Abs, scale=1.0 / WSCALE).then_inc(s["kabs_ev"], 1)
                wait_tile(act, s["kabs_ev"], t)
                nc.scalar.activation(kabs[:, r, :], kabs[:, r, :], ACT.Exp, scale=-1.0).then_inc(s["e1_ev"], 1)
                wait_tile(act, s["e1_ev"], t)
                nc.scalar.activation(kabs[:, r, :], kabs[:, r, :], ACT.Ln, bias=1.0).then_inc(s["l1_ev"], 1)

            def q_exps(t):
                r = t.p % 2
                wait_tile(act, s["qrope_d"], t)
                wait_tile(act, s["qsT_done"], t, 2)
                for h in range(GRP):
                    last = nc.scalar.activation(qe[:, r, h * P:(h + 1) * P], PQ[:, h * P:(h + 1) * P], ACT.Exp,
                                                bias=nqm[:, r, h:h + 1], scale=1.0 / WSCALE,
                                                accum_out=qsum[:, r, h:h + 1])
                last.then_inc(s["q_exp"], 1)

            def decays(t):
                r = t.p % 2
                wait_tile(act, s["small_done"], t)
                nc.scalar.activation(krT[:, 1 - r, :], SM[:, 260:260 + WIN], ACT.Copy)
                wait_tile(act, s["sc_done"], t, 1)
                nc.scalar.activation(krT[:, 2 + r, :], SM[:, 260 + WIN:260 + P], ACT.Copy).then_inc(s["krT_ev"], 1)
                nc.scalar.activation(ked[:, r, :], SM[:, 0:P], ACT.Exp, scale=-1.0)
                wait_tile(act, s["qt_d"], t, 2)
                wait_tile(act, s["sr_d"], t, 1)
                nc.scalar.activation(edT[:, r, :], SM[:, P:P + 130], ACT.Exp).then_inc(s["dec_ev"], 1)

            def copy_qrT(t):
                wait_tile(act, s["qrT_done"], t)
                wait_tile(act, s["sc_done"], t, 2)
                nc.scalar.activation(qrT[:, t.p % 2].rearrange("p b h n -> p h b n"),
                                     X0[:].rearrange("p (h b n) -> p h b n", h=GRP, b=2), ACT.Copy)\
                    .then_inc(s["qrT_ev"], 1)

            def p_exps(t):
                r = t.p % 2
                wait_tile(act, s["npm_d"], t)
                wait_tile(act, s["pt_done"], t, 2)
                for j in range(GRP):
                    last = nc.scalar.activation(pr[:, r, j * P:(j + 1) * P], SC[:, j * P:(j + 1) * P], ACT.Exp,
                                                bias=npm[:, r, j:j + 1], scale=ATT_SCALE,
                                                accum_out=psm[:, r, j:j + 1])
                last.then_inc(s["p_exp"], 1)

            def copy_ktT(t):
                wait_tile(act, s["ktT_done"], t)
                nc.scalar.activation(ktT[:, t.p % 2, :], SM[:, 0:P], ACT.Copy).then_inc(s["ktT_ev"], 1)

            def nf4_abs(t):
                i = t.i
                if t.p == 0:
                    act.wait_ge(s["f_in"], i * 16 + 16)
                    if isinstance(i, int) and i == 0:
                        act.wait_ge(s["f_rest"], 35)
                    else:
                        act.wait_ge(s["f_maxd"], i)
                    nc.scalar.activation(f_abs[:], f_raw[:], ACT.Abs).then_inc(s["f_absd"], 1)

            def split_high(i, job, part):
                src, lo, hi, scaled, high, _, n = part_of(job, part)
                if part == 0:
                    act.wait_ge(s["raw_a"], (job + 1) * 48)
                if part == 3:
                    act.wait_ge(s["raw_b"], (job + 1) * 16)
                nc.scalar.activation(src, src, ACT.Copy, scale=WSCALE).then_inc(scaled, 1)
                if not (isinstance(i, int) and i <= 0):
                    act.wait_ge(s["q_done"] if part < 3 else s["wo_done"], i * STEP)
                act.wait_ge(scaled, n)
                nc.scalar.activation(wh[:, job % 8, lo:hi], src, ACT.Copy).then_inc(high, 1)

            def copy_o(t):
                wait_tile(act, s["o_done"], t)
                wait_tile(act, s["wo_done"], t, 2)
                nc.scalar.activation(oT[:, t.p % 2].rearrange("p h b n -> p b h n"),
                                     PO[:].rearrange("p (b h n) -> p b h n", b=2, h=GRP), ACT.Copy)\
                    .then_inc(s["oT_ev"], 1)

            def turn(t):
                l1, l3 = t.back(1), t.back(3)
                if l3.real():
                    copy_o(l3)
                if l1.real():
                    q_exps(l1)
                    decays(l1)
                if t.real():
                    k_exps(t)
                    nf4_abs(t)
                if l1.real():
                    copy_qrT(l1)
                    p_exps(l1)
                if t.real():
                    split_high(t.i, t.i + NC, t.p)
                if l1.real():
                    copy_ktT(l1)

            for job in range(NC):
                for part in range(4):
                    split_high(-1, job, part)
            act.preload_act_table_set("natural_log_exp_and_others")
            turns(act, 3, turn)

        @block.vector
        def _(dve):
            nc.vector.memset(sr[:], 0.0).then_inc(s["sr_d"], 1)
            dve.wait_ge(s["consts"], 96)
            nc.vector.tensor_copy(identb[:], ident[:]).then_inc(s["z_id"], 1)
            nc.vector.tensor_copy(win[:], f_s[:, 0:2, :]).then_inc(s["z_id"], 1)
            nc.vector.memset(krT[:], 0.0).then_inc(s["z_id"], 1)
            dve.wait_ge(s["z_id"], 5)
            cos_b = lambda t, n: cos[:, t.i % 2, t.p, :].unsqueeze(1).to_broadcast([P, n, P // 2])
            sin_b = lambda t, half, n: sin[:, t.i % 2, t.p, half, :].unsqueeze(1).to_broadcast([P, n, P // 2])

            def rope(t, src, n, dc, ds, done):
                s4 = src.rearrange("p (h a n) -> p h a n", h=n, a=2)
                d4 = ds.rearrange("p (h a n) -> p h a n", h=n, a=2)
                nc.vector.tensor_tensor(dc.rearrange("p (h n) -> p h n", n=P // 2),
                                        src.rearrange("p (h n) -> p h n", n=P // 2), cos_b(t, 2 * n), ALU.mult)
                nc.vector.tensor_tensor(d4[:, :, 0, :], s4[:, :, 1, :], sin_b(t, 0, n), ALU.mult)
                nc.vector.tensor_tensor(d4[:, :, 1, :], s4[:, :, 0, :], sin_b(t, 1, n), ALU.mult).then_inc(done, 1)

            def use_k(t):
                r = t.p % 2
                wait_tile(dve, s["kv_done"], t)
                nc.vector.tensor_reduce(kmx[:, r, :], PKV[:, 0:P], AX.X, ALU.max).then_inc(s["kmx_d"], 1)
                nc.vector.tensor_scalar(kneg[:, r, :], PKV[:, 0:P], 0.0, 1.0 / WSCALE, ALU.min, ALU.mult)\
                    .then_inc(s["kneg_d"], 1)
                wait_tile(dve, s["kmx_d"], t)
                nc.vector.tensor_scalar(nkm[:, r, :], kmx[:, r, :], -1.0 / WSCALE, None, ALU.mult).then_inc(s["nkm_d"], 1)
                wait_tile(dve, s["small_done"], t, 2)
                rope(t, PKV[:, 0:P], 1, kc[:, r, :], ks[:, r, :], s["krope_d"])

            def log_decay(t):
                r = t.p % 2
                wait_tile(dve, s["l1_ev"], t)
                wait_tile(dve, s["kneg_d"], t)
                nc.vector.tensor_tensor(kneg[:, r, :], kneg[:, r, :], kabs[:, r, :], ALU.subtract).then_inc(s["g_d"], 1)

            def use_q(t):
                r = t.p % 2
                wait_tile(dve, s["q_done"], t)
                nc.vector.tensor_reduce(qmx[:, r, :], PQ[:].rearrange("p (h n) -> p h n", h=GRP), AX.X, ALU.max)\
                    .then_inc(s["qmx_d"], 1)
                wait_tile(dve, s["qmx_d"], t)
                nc.vector.tensor_scalar(nqm[:, r, :], qmx[:, r, :], -1.0 / WSCALE, None, ALU.mult).then_inc(s["nqm_d"], 1)
                wait_tile(dve, s["qrT_done"], t, 2)
                rope(t, PQ[:], GRP, qc[:, r, :], qs[:, r, :], s["qrope_d"])

            def gla_k(t):
                r = t.p % 2
                wait_tile(dve, s["ke_ev"], t)
                nc.vector.reciprocal(rks[:, r, :], ksum[:, r, :]).then_inc(s["rks_d"], 1)
                wait_tile(dve, s["rks_d"], t)
                wait_tile(dve, s["dec_ev"], t)
                wait_tile(dve, s["u_done"], t, 2)
                nc.vector.scalar_tensor_tensor(out=kt[:, r, :], in0=ke[:, r, :], scalar=rks[:, r, :], in1=ked[:, r, :],
                                               op0=ALU.mult, op1=ALU.mult).then_inc(s["kt_d"], 1)

            def gla_q(t):
                r = t.p % 2
                wait_tile(dve, s["qsT_done"], t)
                wait_tile(dve, s["dec_ev"], t)
                wait_tile(dve, s["o_done"], t, 2)
                nc.vector.tensor_tensor(qtT[:, r].rearrange("p h b n -> p h (b n)"),
                                        X0[:].rearrange("p (h n) -> p h n", h=GRP),
                                        edT[:, r, 0:P].unsqueeze(1).to_broadcast([P, GRP, P]), ALU.mult)\
                    .then_inc(s["qt_d"], 1)

            def q_sums(t):
                r = t.p % 2
                wait_tile(dve, s["q_exp"], t)
                wait_tile(dve, s["qn_p"], t, 2)
                nc.vector.reciprocal(rq[:, r, :], qsum[:, r, :]).then_inc(s["rq_d"], 1)

            def p_max(t):
                r = t.p % 2
                wait_tile(dve, s["sc_done"], t)
                nc.vector.tensor_reduce(pmx[:, r, :], SC[:].rearrange("p (h n) -> p h n", h=GRP), AX.X, ALU.max)\
                    .then_inc(s["pmx_d"], 1)
                wait_tile(dve, s["pmx_d"], t)
                nc.vector.tensor_scalar(npm[:, r, :], pmx[:, r, :], -ATT_SCALE, None, ALU.mult).then_inc(s["npm_d"], 1)

            def p_sums(t):
                r = t.p % 2
                wait_tile(dve, s["p_exp"], t)
                wait_tile(dve, s["pn_p"], t, 2)
                nc.vector.reciprocal(rp[:, r, :], psm[:, r, :]).then_inc(s["rp_d"], 1)

            def mask_gla(t):
                wait_tile(dve, s["at_done"], t)
                wait_tile(dve, s["pa_d"], t, 1)
                nc.vector.tensor_tensor(am[:], X1[:], cau[:], ALU.mult).then_inc(s["am_d"], 1)

            def add_gla(t):
                wait_tile(dve, s["pt_done"], t)
                wait_tile(dve, s["am_d"], t)
                wait_tile(dve, s["o_done"], t, 2)
                nc.vector.tensor_tensor(pa[:, t.p % 2, :], X1[:], am[:], ALU.add).then_inc(s["pa_d"], 1)

            def state(t):
                r, nxt = t.p % 2, t.back(-1)
                wait_tile(dve, s["u_done"], t)
                nc.vector.tensor_tensor(su[:], SM[:, 0:P], sr[:, r, :], ALU.add).then_inc(s["su_d"], 1)
                if not nxt.real():
                    return
                wait_tile(dve, s["dec_ev"], nxt)
                scale = edT[:, 1 - r, P:P + 1]
                if nxt.p == 0:
                    nc.vector.tensor_tensor(em[:, 0, :], scale, keep[:, nxt.i % 2:nxt.i % 2 + 1] if isinstance(nxt.i, int)
                                            else keep[:].unsqueeze(2)[:, nxt.i % 2, :], ALU.mult).then_inc(s["em_d"], 1)
                    dve.wait_ge(s["em_d"], nxt.i)
                    scale = em[:, 0, :]
                wait_tile(dve, s["su_d"], t)
                nc.vector.tensor_scalar(sr[:, 1 - r, :], su[:], edT[:, r, P - 1:P], scale, ALU.mult, ALU.mult)\
                    .then_inc(s["sr_d"], 1)

            def add_out(t):
                wait_tile(dve, s["wo_done"], t)
                a = acc[:].rearrange("p (g q) n -> p g q n", q=STEP)[:, t_index(t), t.p, :]
                nc.vector.tensor_tensor(a, PW[:], a, ALU.add).then_inc(s["acc_d"], 1)

            def nf4(t):
                i = t.i
                if t.p == 0:
                    dve.wait_ge(s["f_in"], i * 16 + 16)
                    raw3 = f_raw[:].rearrange("p (b n) -> p b n", n=BLK)
                    dve.wait_ge(s["f_absd"], i + 1)
                    fmax = f_max[:, i % 2, :]
                    nc.vector.tensor_reduce(fmax, f_abs[:].rearrange("p (b n) -> p b n", n=BLK), AX.X, ALU.max)\
                        .then_inc(s["f_maxd"], 1)
                    dve.wait_ge(s["f_maxd"], i + 1)
                    nc.vector.scalar_tensor_tensor(out=f_safe[:], in0=fmax, scalar=0.0, in1=fmax,
                                                   op0=ALU.is_equal, op1=ALU.add).then_inc(s["f_safed"], 1)
                    dve.wait_ge(s["f_safed"], i + 1)
                    nc.vector.reciprocal(f_rec[:], f_safe[:]).then_inc(s["f_recd"], 1)
                    dve.wait_ge(s["f_recd"], i + 1)
                    nc.vector.tensor_tensor(f_nrm[:].rearrange("p (b n) -> p b n", n=BLK), raw3,
                                            f_rec[:].unsqueeze(2).to_broadcast([P, NF4_PIECE // BLK, BLK]), ALU.mult)\
                        .then_inc(s["f_nrmd"], 1)
                    dve.wait_ge(s["f_nrmd"], i + 1)
                for k in NF4_STEPS[t.p]:
                    if k >= 8:
                        dve.wait_ge(s["f_ad"], i * 14 + max(k - 8, 1))
                    elif not (isinstance(i, int) and i == 0):
                        dve.wait_ge(s["f_ad"], i * 14 - (6 - k if k < 7 else 0))
                    nc.vector.tensor_scalar(f_s[:, k % 8, :], f_nrm[:], float(BOUND[k]), float(DELTA[k]),
                                            ALU.is_gt, ALU.mult).then_inc(s["f_sd"], 1)

            def nf4_end(i):
                dve.wait_ge(s["f_ad"], i * 14 + 14)
                if isinstance(i, int) and i == 0:
                    dve.wait_ge(s["f_rout"], 16)
                else:
                    dve.wait_ge(s["f_out"], i * 16)
                nc.vector.scalar_tensor_tensor(
                    out=f_dq[:].rearrange("p (b n) -> p b n", n=BLK), in0=f_acc[:].rearrange("p (b n) -> p b n", n=BLK),
                    scalar=float(CODE[0]), in1=f_max[:, i % 2, :].unsqueeze(2).to_broadcast([P, NF4_PIECE // BLK, BLK]),
                    op0=ALU.add, op1=ALU.mult).then_inc(s["f_dqd"], 1)

            def turn(t):
                l1, l2, l3 = t.back(1), t.back(2), t.back(3)
                if t.real():
                    use_k(t)
                if l1.real():
                    q_sums(l1)
                if t.p == 1 and not (isinstance(t.i, int) and t.i == 0):
                    nf4_end(t.i - 1)
                if l2.real():
                    mask_gla(l2)
                if l1.real():
                    gla_k(l1)
                if l3.real():
                    add_out(l3)
                if t.real():
                    log_decay(t)
                if l2.real():
                    state(l2)
                    add_gla(l2)
                if l1.real():
                    p_max(l1)
                if t.real():
                    nf4(t)
                if l1.real():
                    p_sums(l1)
                if t.real():
                    use_q(t)
                if l1.real():
                    gla_q(l1)

            def nf4_rest():
                n = NF4_REST
                b = n // BLK
                blocks = lambda a: a[:, 0:n].rearrange("p (b n) -> p b n", n=BLK)
                spread = lambda a: a[:, 0:b].unsqueeze(2).to_broadcast([P, b, BLK])
                done = 0

                def then(ins):
                    nonlocal done
                    done += 1
                    ins.then_inc(s["f_rest"], 1)
                    dve.wait_ge(s["f_rest"], done)

                dve.wait_ge(s["f_rin"], 16)
                then(nc.vector.scalar_tensor_tensor(out=f_abs[:, 0:n], in0=f_dq[:, 0:n], scalar=-1.0, in1=f_dq[:, 0:n],
                                                    op0=ALU.mult, op1=ALU.max))
                then(nc.vector.tensor_reduce(f_max[:, 1, 0:b], blocks(f_abs), AX.X, ALU.max))
                then(nc.vector.scalar_tensor_tensor(out=f_safe[:, 0:b], in0=f_max[:, 1, 0:b], scalar=0.0,
                                                    in1=f_max[:, 1, 0:b], op0=ALU.is_equal, op1=ALU.add))
                then(nc.vector.reciprocal(f_rec[:, 0:b], f_safe[:, 0:b]))
                then(nc.vector.tensor_tensor(blocks(f_nrm), blocks(f_dq), spread(f_rec), ALU.mult))
                then(nc.vector.tensor_scalar(f_acc[:, 0:n], f_nrm[:, 0:n], float(BOUND[0]), float(DELTA[0]),
                                             ALU.is_gt, ALU.mult))
                for k in range(1, 15):
                    then(nc.vector.tensor_scalar(f_abs[:, 0:n], f_nrm[:, 0:n], float(BOUND[k]), float(DELTA[k]),
                                                 ALU.is_gt, ALU.mult))
                    then(nc.vector.tensor_tensor(f_acc[:, 0:n], f_acc[:, 0:n], f_abs[:, 0:n], ALU.add))
                then(nc.vector.scalar_tensor_tensor(out=blocks(f_dq), in0=blocks(f_acc), scalar=float(CODE[0]),
                                                    in1=spread(f_max[:, 1]), op0=ALU.add, op1=ALU.mult))

            nf4_rest()
            turns(dve, 3, turn)

        @block.tensor
        def _(pe):
            pe.wait_ge(s["consts"], 96)
            pe.wait_ge(s["z_id"], 5)
            slot = lambda t: (t.i // NC) % 2 * NC

            def decays_and_krT(t):
                r = t.p % 2
                wait_tile(pe, s["g_d"], t)
                wait_tile(pe, s["krope_p"], t)
                wait_tile(pe, s["ktT_ev"], t, 1)
                nc.tensor.matmul(SM[:, 0:P], cum[:, 0:P], kneg[:, r, :], start=True, stop=True)
                nc.tensor.matmul(SM[:, P:P + 130], kneg[:, r, :], cum[:], start=True, stop=True)
                nc.tensor.transpose(SM[:, 260:260 + P], kc[:, r, :], ident[:]).then_inc(s["small_done"], 1)

            def turn_q(t):
                r = t.p % 2
                wait_tile(pe, s["qrope_p"], t)
                wait_tile(pe, s["qt_d"], t, 1)
                for h in range(GRP):
                    last = nc.tensor.transpose(X0[:, h * P:(h + 1) * P], qc[:, r, h * P:(h + 1) * P], ident[:])
                last.then_inc(s["qrT_done"], 1)

            def gla_scores(t):
                r = t.p % 2
                wait_tile(pe, s["qt_d"], t)
                wait_tile(pe, s["ktT_ev"], t)
                wait_tile(pe, s["pa_d"], t, 1)
                nc.tensor.matmul(X1[:], ktT[:, r, :], qtT[:, r].rearrange("p h b n -> p b h n"),
                                 start=True, stop=True).then_inc(s["at_done"], 1)

            def project_out(t):
                if t.p == 0:
                    pe.wait_ge(s["wo_lo"], t.i + NC)
                wait_tile(pe, s["oT_ev"], t)
                wait_tile(pe, s["acc_d"], t, 1)
                sl = slot(t)
                for h in range(GRP):
                    for k, w in enumerate((wh, wl)):
                        last = nc.tensor.matmul(PW[:], oT[:, t.p % 2, h].rearrange("p b n -> p (b n)"),
                                                w[:, sl + h, QW + KVW:WW],
                                                start=(h == 0 and k == 0), stop=(h == GRP - 1 and k == 1))
                last.then_inc(s["wo_done"], 1)

            def project(t, dst, lo, hi, done):
                sl = slot(t)
                n = 0
                for c in range(NC):
                    for a, w in ((xh, wh), (xh, wl), (xl, wh)):
                        av = a[:].rearrange("p c (g q) n -> p c g q n", q=STEP)[:, c, t_index(t), t.p, :]
                        last = nc.tensor.matmul(dst, av, w[:, sl + c, lo:hi], start=(n == 0), stop=(n == 3 * NC - 1))
                        n += 1
                last.then_inc(done, 1)

            def project_q(t):
                wait_tile(pe, s["q_exp"], t, 1)
                project(t, PQ[:], 0, QW, s["q_done"])

            def project_kv(t):
                if t.p == 0:
                    pe.wait_ge(s["wqk_lo"], (t.i + NC) * 3)
                wait_tile(pe, s["kabs_ev"], t, 1)
                project(t, PKV[:, 0:KVW], QW, QW + KVW, s["kv_done"])

            def scores(t):
                r = t.p % 2
                wait_tile(pe, s["krT_ev"], t)
                wait_tile(pe, s["qrT_ev"], t)
                wait_tile(pe, s["p_exp"], t, 1)
                nc.tensor.matmul(SC[:], identb[:], win[:, 1, :] if t.p else win[:, t.i % 2, :], start=True, stop=False)
                low = 1 - r
                for b in range(2):
                    high = 2 + r if b else 3 - r
                    keys = krT[:, low:high + 1:high - low, :]
                    for hp in range(2):
                        j = 2 * b + hp
                        last = nc.tensor.matmul(SC[:, j * P:(j + 1) * P], 
                                                qrT[:, r, b, 2 * hp:2 * hp + 2, :].rearrange("p h n -> p (h n)"), keys,
                                                start=False, stop=(j == 3))
                last.then_inc(s["sc_done"], 1)

            def probabilities(t):
                r = t.p % 2
                wait_tile(pe, s["pn_p"], t)
                wait_tile(pe, s["am_d"], t)
                for j in range(GRP):
                    last = nc.tensor.transpose(X1[:, j * P:(j + 1) * P], pr[:, r, j * P:(j + 1) * P], ident[:])
                last.then_inc(s["pt_done"], 1)

            def inter_and_update(t):
                r = t.p % 2
                wait_tile(pe, s["sr_d"], t)
                wait_tile(pe, s["oT_ev"], t, 1)
                nc.tensor.matmul(PO[:], sr[:, r, :], qtT[:, r].rearrange("p h b n -> p b h n"), start=True, stop=False)
                if t.back(-1).real():
                    wait_tile(pe, s["dec_ev"], t.back(-1))
                nc.tensor.matmul(SM[:, 0:P], kt[:, r, :], va[:, t.p, :], start=True, stop=True).then_inc(s["u_done"], 1)

            def qsT_and_ktT(t):
                r = t.p % 2
                wait_tile(pe, s["qn_p"], t)
                wait_tile(pe, s["qrT_ev"], t)
                for h in range(GRP):
                    last = nc.tensor.transpose(X0[:, h * P:(h + 1) * P], qe[:, r, h * P:(h + 1) * P], ident[:])
                last.then_inc(s["qsT_done"], 1)
                wait_tile(pe, s["kt_d"], t)
                wait_tile(pe, s["su_d"], t, 1)
                nc.tensor.transpose(SM[:, 0:P], kt[:, r, :], ident[:]).then_inc(s["ktT_done"], 1)

            def output(t):
                r = t.p % 2
                wait_tile(pe, s["pa_d"], t)
                wait_tile(pe, s["v_ev"], t)
                for b, v in enumerate((vm, va)):
                    last = nc.tensor.matmul(PO[:, b * 256:(b + 1) * 256], v[:, t.p, :], pa[:, r, b * 256:(b + 1) * 256],
                                            start=False, stop=(b == 1))
                last.then_inc(s["o_done"], 1)

            def turn(t):
                l1, l2, l3 = t.back(1), t.back(2), t.back(3)
                if t.real():
                    project_kv(t)
                if l1.real():
                    decays_and_krT(l1)
                if l2.real():
                    gla_scores(l2)
                if l3.real():
                    project_out(l3)
                if l1.real():
                    turn_q(l1)
                if l2.real():
                    inter_and_update(l2)
                    probabilities(l2)
                if l1.real():
                    scores(l1)
                if t.real():
                    project_q(t)
                if l1.real():
                    qsT_and_ktT(l1)
                if l2.real():
                    output(l2)

            turns(pe, 3, turn)


def ffn(nc, sem, bank, rows, xh, xl, ident, st, mv, sd, rs, x_rows, out_rows, dq):
    with ExitStack() as ctx:
        def sb(name, shape, dt=F32):
            return ctx.enter_context(nc.sbuf_tensor(name, shape, dt))

        w12h = sb("w12h", [P, NC, 2 * FFN], F16)
        w12l = sb("w12l", [P, NC, 2 * FFN], F16)
        w3h = sb("w3h", [P, FC, HID], F16)
        w3l = sb("w3l", [P, FC, HID], F16)
        xr = sb("xr", [P, 4, HID])
        xn = sb("xn3", [P, 2, HID])
        wt = sb("wt", [P, 4, HID])

        r = {n: sem("res_" + n) for n in ("st", "mv", "var", "sd", "rs", "z", "x1")}
        r_in = [sem(f"res_in{j}") for j in range(4)]
        with nc.Block() as block:

            @block.sync
            def _(sp):
                for t in range(TILES):
                    if t >= 4:
                        sp.wait_ge(r["x1"], t - 3)
                    sp.dma_start(xr[:, t % 4, :], x_rows[:, t, :]).then_inc(r_in[t % 4], 16)

            @block.scalar
            def _(act):
                act.wait_ge(r["var"], 1)
                nc.scalar.activation(sd[:, :], sd[:, :], ACT.Sqrt).then_inc(r["sd"], 1)

            @block.vector
            def _(dve):
                for t in range(TILES):
                    nc.vector.bn_stats(st[:, t, :], rows[:, t, :]).then_inc(r["st"], 1)
                for t in range(TILES):
                    dve.wait_ge(r["st"], t + 1)
                    nc.vector.bn_aggr(mv[:, t, :], st[:, t, :]).then_inc(r["mv"], 1)
                dve.wait_ge(r["mv"], TILES)
                nc.vector.tensor_scalar(sd[:, :], mv[:, :, 1], EPS * WSCALE * WSCALE, None, ALU.add).then_inc(r["var"], 1)
                dve.wait_ge(r["sd"], 1)
                nc.vector.reciprocal(rs[:, :], sd[:, :]).then_inc(r["rs"], 1)
                dve.wait_ge(r["rs"], 1)
                for t in range(TILES):
                    nc.vector.tensor_scalar(rows[:, t, :], rows[:, t, :], mv[:, t, 0:1], rs[:, t:t + 1],
                                            ALU.subtract, ALU.mult).then_inc(r["z"], 1)
                    dve.wait_ge(r_in[t % 4], 16 * (t // 4 + 1))
                    dve.wait_ge(r["z"], t + 1)
                    nc.vector.tensor_tensor(rows[:, t, :], rows[:, t, :], xr[:, t % 4, :], ALU.add).then_inc(r["x1"], 1)

        s3 = [sem("ln3_" + n) for n in ("st", "mv", "var", "sd", "rs", "xn", "tp", "hi", "lo")]
        with nc.Block() as block:
            norm_tiles(block, nc, rows, (st, mv, sd, rs), xn, xh, xl, ident, bank, s3,
                       lambda t: (r["x1"], t + 1))

        w12_v = dq[0:2 * FFN * HID].rearrange("(r n) -> r n", n=HID)
        w3_v = dq[2 * FFN * HID:].rearrange("(r n) -> r n", n=FFN)
        jobs = []
        for j in range(0, 2 * FFN, P):
            m = min(P, 2 * FFN - j)
            jobs.append((w12_v[j:j + m, :], m, [P] * NC, P, [w[:, :, j:j + m] for w in (w12h, w12l)]))
        for j in range(HID // P):
            for h0 in (0, 4):
                jobs.append((w3_v[j * P:(j + 1) * P, h0 * P:(h0 + 4) * P], P, [P] * 4, P,
                             [w[:, h0:h0 + 4, j * P:(j + 1) * P] for w in (w3h, w3l)]))
            jobs.append((w3_v[j * P:(j + 1) * P, 8 * P:10 * P], P, [P] * 2, P,
                         [w[:, 8:10, j * P:(j + 1) * P] for w in (w3h, w3l)]))
            jobs.append((w3_v[j * P:(j + 1) * P, 10 * P:FFN], P, [FLAST], FLAST,
                         [w[0:FLAST, 10:11, j * P:(j + 1) * P] for w in (w3h, w3l)]))
        w = {n: sem("wt_" + n) for n in ("tp", "hi", "lo")}
        w_in = [sem(f"wt_in{j}") for j in range(4)]
        with nc.Block() as block:

            def shown(j):
                _, m, cols, out_p, _ = jobs[j]
                return bank[j % 4][0:out_p, 0:len(cols) * m].rearrange("p (c n) -> p c n", n=m)

            @block.sync
            def _(sp):
                for j, (src, m, cols, _, _) in enumerate(jobs):
                    if j >= 4:
                        sp.wait_ge(w["tp"], j - 3)
                    sp.dma_start(wt[0:m, j % 4, 0:sum(cols)], src).then_inc(w_in[j % 4], 16)

            @block.tensor
            def _(pe):
                for j, (_, m, cols, out_p, _) in enumerate(jobs):
                    pe.wait_ge(w_in[j % 4], 16 * (j // 4 + 1))
                    if j >= 4:
                        pe.wait_ge(w["lo"], j - 3)
                    at = 0
                    for c, n in enumerate(cols):
                        last = nc.tensor.transpose(bank[j % 4][0:n, c * m:(c + 1) * m], wt[0:m, j % 4, at:at + n],
                                                   ident[0:m, 0:m])
                        at += n
                    last.then_inc(w["tp"], 1)

            @block.scalar
            def _(act):
                for j in range(len(jobs)):
                    act.wait_ge(w["tp"], j + 1)
                    nc.scalar.activation(jobs[j][4][0], shown(j), ACT.Copy, scale=WSCALE).then_inc(w["hi"], 1)

            @block.vector
            def _(dve):
                for j in range(len(jobs)):
                    dve.wait_ge(w["hi"], j + 1)
                    nc.vector.scalar_tensor_tensor(out=jobs[j][4][1], in0=shown(j), scalar=WSCALE, in1=jobs[j][4][0],
                                                   op0=ALU.mult, op1=ALU.subtract).then_inc(w["lo"], 1)

        sg = sb("sg", [P, 2, 512])
        hf = sb("hf", [P, 2, 512])
        hh = sb("hh", [P, 2, 512], F16)
        hl = sb("hl", [P, 2, 512], F16)
        yo = sb("yo", [P, STEP, HID])
        yst = sb("yst", [P, STEP, 6])
        ymv = sb("ymv", [P, STEP, 2])
        ysd = sb("ysd", [P, STEP])
        yrs = sb("yrs", [P, STEP])
        f = {n: sem("ffn_" + n) for n in ("gate", "up", "sg", "hf", "hh", "hl", "y", "st", "mv", "var", "sd", "rs", "z",
                                          "o")}
        f_out = [sem(f"ffn_out{q}") for q in range(STEP)]
        G, U, Y = bank[0:2], bank[2:4], bank[4:8]
        with nc.Block() as block:

            def groups(eng, group):
                group(0)
                with eng.Fori(1, TILES // STEP) as g:
                    group(g)

            def after(eng, sm, per, g, n):
                v = g * per + n
                if isinstance(v, int) and v <= 0:
                    return
                eng.wait_ge(sm, v)

            width = lambda c: P if c < FC - 1 else FLAST

            @block.tensor
            def _(pe):
                def hidden(g, c):
                    n = width(c)
                    b = c % 2
                    for dst, off, free, done in ((G[b], 0, "hf", "gate"), (U[b], FFN, "hf", "up")):
                        after(pe, f["hf"], FC, g, c - 1 if c >= 2 else (0 if c == 0 else -1))
                        k = 0
                        for d in range(NC):
                            for a, ww in ((xh, w12h), (xl, w12h), (xh, w12l)):
                                x4 = a[:].rearrange("p c (g q) n -> p c g (q n)", q=STEP)[:, d, g, :]
                                last = nc.tensor.matmul(dst[0:n, :], ww[:, d, off + c * P:off + c * P + n], x4,
                                                        start=(k == 0), stop=(k == 3 * NC - 1))
                                k += 1
                        last.then_inc(f[done], 1)

                def down(g, c):
                    n = width(c)
                    after(pe, f["hl"], FC, g, c + 1)
                    if c == 0:
                        after(pe, f["z"], STEP, g, 0)
                    for q in range(STEP):
                        for k, (a, ww) in enumerate(((hh, w3h), (hh, w3l), (hl, w3h))):
                            last = nc.tensor.matmul(Y[q][:], a[0:n, c % 2, q * P:(q + 1) * P], ww[0:n, c, :],
                                                    start=(c == 0 and k == 0), stop=(c == FC - 1 and k == 2))
                    last.then_inc(f["y"], 1)

                def group(g):
                    hidden(g, 0)
                    for c in range(1, FC):
                        hidden(g, c)
                        down(g, c - 1)
                    down(g, FC - 1)

                groups(pe, group)

            @block.scalar
            def _(act):
                def group(g):
                    for c in range(FC):
                        n = width(c)
                        after(act, f["gate"], FC, g, c + 1)
                        after(act, f["hf"], FC, g, c - 1)
                        nc.scalar.activation(sg[0:n, c % 2, :], G[c % 2][0:n, :], ACT.Silu, scale=1.0 / WSCALE)\
                            .then_inc(f["sg"], 1)
                        after(act, f["hf"], FC, g, c + 1)
                        after(act, f["y"], FC, g, c - 1)
                        nc.scalar.activation(hh[0:n, c % 2, :], hf[0:n, c % 2, :], ACT.Copy).then_inc(f["hh"], 1)
                    after(act, f["var"], 1, g, 1)
                    nc.scalar.activation(ysd[:, :], ysd[:, :], ACT.Sqrt).then_inc(f["sd"], 1)

                groups(act, group)

            @block.vector
            def _(dve):
                def group(g):
                    for c in range(FC):
                        n = width(c)
                        after(dve, f["sg"], FC, g, c + 1)
                        after(dve, f["up"], FC, g, c + 1)
                        after(dve, f["hl"], FC, g, c - 1)
                        nc.vector.scalar_tensor_tensor(out=hf[0:n, c % 2, :], in0=U[c % 2][0:n, :],
                                                       scalar=HSCALE / WSCALE, in1=sg[0:n, c % 2, :],
                                                       op0=ALU.mult, op1=ALU.mult).then_inc(f["hf"], 1)
                    after(dve, f["y"], FC, g, FC)
                    for q in range(STEP):
                        nc.vector.bn_stats(yst[:, q, :], Y[q][:]).then_inc(f["st"], 1)
                    after(dve, f["st"], STEP, g, STEP)
                    nc.vector.memset(ysd[:, :], 0.0)
                    for q in range(STEP):
                        nc.vector.bn_aggr(ymv[:, q, :], yst[:, q, :]).then_inc(f["mv"], 1)
                    after(dve, f["mv"], STEP, g, STEP)
                    nc.vector.tensor_scalar(ysd[:, :], ymv[:, :, 1], EPS * (WSCALE * HSCALE) ** 2, None, ALU.add)\
                        .then_inc(f["var"], 1)
                    after(dve, f["sd"], 1, g, 1)
                    nc.vector.reciprocal(yrs[:, :], ysd[:, :]).then_inc(f["rs"], 1)
                    after(dve, f["rs"], 1, g, 1)
                    for q in range(STEP):
                        after(dve, f_out[q], 16, g, 0)
                        nc.vector.tensor_scalar(yo[:, q, :], Y[q][:], ymv[:, q, 0:1], yrs[:, q:q + 1],
                                                ALU.subtract, ALU.mult).then_inc(f["z"], 1)
                        after(dve, f["z"], STEP, g, q + 1)
                        rw = rows[:].rearrange("p (g q) n -> p g q n", q=STEP)[:, g, q, :]
                        nc.vector.tensor_tensor(yo[:, q, :], yo[:, q, :], rw, ALU.add).then_inc(f["o"], 1)

                groups(dve, group)

            @block.gpsimd
            def _(pool):
                def group(g):
                    for c in range(FC):
                        n = width(c)
                        after(pool, f["hh"], FC, g, c + 1)
                        after(pool, f["y"], FC, g, c - 1)
                        nc.gpsimd.tensor_tensor(hl[0:n, c % 2, :], hf[0:n, c % 2, :], hh[0:n, c % 2, :], ALU.subtract)\
                            .then_inc(f["hl"], 1)

                groups(pool, group)

            @block.sync
            def _(sp):
                def group(g):
                    for q in range(STEP):
                        after(sp, f["o"], STEP, g, q + 1)
                        out4 = out_rows.rearrange("p (g q) n -> p g q n", q=STEP)
                        sp.dma_start(out4[:, g, q, :], yo[:, q, :]).then_inc(f_out[q], 16)
                groups(sp, group)
                for q in range(STEP):
                    sp.wait_ge(f_out[q], 16 * (TILES // STEP))


def constants():
    half = np.arange(P // 2, dtype=np.float32)
    inv = (np.float32(1.0) / np.power(np.float32(10000.0), np.float32(2.0) * half / np.float32(P))).astype(np.float32)
    fr = np.arange(SEQ, dtype=np.float32)[:, None] * inv[None, :]
    lay = lambda a: np.ascontiguousarray(a.reshape(TPB, P, P // 2).transpose(1, 0, 2).reshape(P, 2, STEP, P // 2))
    cos = lay(np.cos(fr).astype(np.float32) / np.float32(WSCALE))
    sn = lay(np.sin(fr).astype(np.float32) / np.float32(WSCALE))
    sin = np.ascontiguousarray(np.stack([-sn, sn], axis=3))
    a = np.arange(P)[:, None] % WIN
    slot = np.arange(P)[None, :]
    win = np.zeros((P, 2, 2, 2, P), np.float32)
    c0 = np.where(slot < WIN, slot + WIN, slot - WIN)
    c1 = slot
    for ver in range(2):
        for b, c in enumerate((c0, c1)):
            ok = (a + WIN - c >= 0) & (a + WIN - c <= WIN)
            if ver == 0 and b == 0:
                ok = ok & (c >= WIN)
            win[:, ver, b, :, :] = np.where(ok, 0.0, MASKED)[:, None, :]
    win = np.ascontiguousarray(win.reshape(P, 2, 512))
    j = np.arange(P)[:, None]
    i = np.arange(P)[None, :]
    cau = (j <= i).astype(np.float32).reshape(P, 2, 1, WIN)
    cau = np.ascontiguousarray(np.broadcast_to(cau, (P, 2, GRP, WIN)).reshape(P, 512))
    mid = P // 2 - 1
    cum = np.zeros((P, 130), np.float32)
    cum[:, 0:P] = ((j > mid) & (j <= i)).astype(np.float32) - ((j <= mid) & (j > i)).astype(np.float32)
    cum[:, P] = (np.arange(P) <= mid)
    cum /= 16.0
    keep = np.ones((P, 2), np.float32)
    keep[:, 0] = 0.0
    return {"cosc": cos, "sinc": sin, "winmask": win, "causal": cau, "cumsum": cum,
            "identc": np.eye(P, dtype=np.float32), "keepc": keep}


def kernel(L0_attn_hidden_states, L0_attn_Wq, L0_attn_Wk, L0_attn_Wv, L0_attn_Wo, L0_ffn_w1, L0_ffn_w2, L0_ffn_w3):
    import concourse.bacc as _bacc
    from concourse.bass_utils import run_bass_kernel_spmd as _run

    nc = _bacc.Bacc("TRN2", target_bir_lowering=False, num_devices=1)
    arrays = {
        "x": L0_attn_hidden_states, "wq": L0_attn_Wq, "wk": L0_attn_Wk, "wv": L0_attn_Wv, "wo": L0_attn_Wo,
        "wf": np.concatenate([np.asarray(w).reshape(-1) for w in (L0_ffn_w1, L0_ffn_w2, L0_ffn_w3)]),
    }
    arrays = {k: np.ascontiguousarray(v) for k, v in arrays.items()}
    arrays.update(constants())
    args = [nc.dram_tensor(k, v.shape, mybir.dt.from_np(v.dtype), kind="ExternalInput").ap() for k, v in arrays.items()]
    dq = nc.dram_tensor("dequantised", (3 * FFN * HID,), F32, kind="Internal").ap()
    out = nc.dram_tensor("out", (BATCH, SEQ, HID), F32, kind="ExternalOutput").ap()
    layer(nc, *args, dq, out)
    return _run(nc, [arrays], core_ids=[0]).results[0]["out"]
```

```python
from contextlib import ExitStack

import numpy as np
import concourse.bass as bass
from concourse import mybir

F32 = mybir.dt.float32
F16 = mybir.dt.float16
BF16 = mybir.dt.bfloat16
ALU = mybir.AluOpType
ACT = mybir.ActivationFunctionType
AX = mybir.AxisListType

P = 128
HID = 512
NC = HID // P
HEADS, KVH = 32, 8
GRP = HEADS // KVH
BATCH, SEQ, WIN = 2, 1024, 64
TILES = BATCH * SEQ // P
TPB = SEQ // P
STEP = 4
TURNS = KVH * TILES
STEPS = TURNS // STEP
FFN = 1376
FC = (FFN + P - 1) // P
FLAST = FFN - (FC - 1) * P
QW = GRP * P
KVW = 2 * P
WW = QW + KVW + HID
WSCALE = 256.0
HSCALE = 16.0
ATT_SCALE = float(P) ** -0.5
EPS = 1e-5
MASKED = -1e30
BLK = 64
NF4_COLS = 3 * FFN * HID // P
NF4_PIECE = 512
NF4_REST = NF4_COLS - STEPS * NF4_PIECE
NF4_STEPS = (range(0, 2), range(2, 6), range(6, 11), range(11, 15))
CODE = np.array([-1.0, -0.6961928009986877, -0.5250730514526367, -0.39491748809814453,
                 -0.28444138169288635, -0.18477343022823334, -0.09105003625154495, 0.0,
                 0.07958029955625534, 0.16093020141124725, 0.24611230194568634, 0.33791524171829224,
                 0.44070982933044434, 0.5626170039176941, 0.7229568362236023, 1.0], np.float32)
BOUND = ((CODE[:-1] + CODE[1:]) * np.float32(0.5)).astype(np.float32)
DELTA = (CODE[1:] - CODE[:-1]).astype(np.float32)


class Tile:

    def __init__(self, i, p):
        self.i, self.p = i, p

    def real(self):
        return not isinstance(self.i, int) or 0 <= STEP * self.i + self.p < TURNS

    def back(self, lag):
        q = self.p - lag
        return Tile(self.i + q // STEP, q % STEP) if q // STEP else Tile(self.i, q)

    def count(self):
        return self.i * STEP + (self.p + 1)


def wait_tile(eng, sem, t, back=0):
    v = t.count() - back
    if isinstance(v, int) and v <= 0:
        return
    eng.wait_ge(sem, v)


def turns(eng, last_lag, turn):
    for p in range(STEP):
        turn(Tile(0, p))
    with eng.Fori(1, STEPS) as i:
        for p in range(STEP):
            turn(Tile(i, p))
    for p in range(last_lag):
        turn(Tile(STEPS, p))


def layer(nc, x, wq, wk, wv, wo, wf, cosc, sinc, winmask, causal, cumsum, identc, keepc, dq, out):
    x_rows = x.rearrange("b (t p) d -> p (b t) d", p=P)
    out_rows = out.rearrange("b (t p) d -> p (b t) d", p=P)
    wq_v = wq.rearrange("(c p) (k n) -> c k p n", p=P, n=QW)
    wk_v = wk.rearrange("(c p) (k n) -> c k p n", p=P, n=P)
    wv_v = wv.rearrange("(c p) (k n) -> c k p n", p=P, n=P)
    wo_v = wo.rearrange("(k c p) n -> c k p n", p=P, c=GRP)
    wf_v = wf.rearrange("(p n) -> p n", p=P)
    dq_v = dq.rearrange("(p n) -> p n", p=P)
    wf_p = wf_v[:, 0:STEPS * NF4_PIECE].rearrange("p (i n) -> p i n", n=NF4_PIECE)
    dq_p = dq_v[:, 0:STEPS * NF4_PIECE].rearrange("p (i n) -> p i n", n=NF4_PIECE)

    with ExitStack() as whole:
        def sbw(name, shape, dt):
            return whole.enter_context(nc.sbuf_tensor(name, shape, dt))

        def sem(name):
            return whole.enter_context(nc.semaphore(name))

        xh = sbw("xh", [P, NC, TILES, P], F16)
        xl = sbw("xl", [P, NC, TILES, P], F16)
        rows = sbw("rows", [P, TILES, HID], F32)
        ident = sbw("ident", [P, P], F32)
        bank = [whole.enter_context(nc.psum_tensor(f"bank{j}", [P, 512], F32)) for j in range(8)]
        st = sbw("st", [P, TILES, 6], F32)
        mv = sbw("mv", [P, TILES, 2], F32)
        sd = sbw("sd", [P, TILES], F32)
        rs = sbw("rs", [P, TILES], F32)

        attention(nc, sem, bank, rows, xh, xl, ident, (st, mv, sd, rs), x_rows, wq_v, wk_v, wv_v, wo_v, wf_v, wf_p,
                  dq_v, dq_p, cosc, sinc, winmask, causal, cumsum, identc, keepc)
        ffn(nc, sem, bank, rows, xh, xl, ident, (st, mv, sd, rs), x_rows, out_rows, dq)


def attention(nc, sem, bank, rows, xh, xl, ident, stats, x_rows, wq_v, wk_v, wv_v, wo_v, wf_v, wf_p, dq_v, dq_p,
              cosc, sinc, winmask, causal, cumsum, identc, keepc):
    with ExitStack() as ctx:
        def sb(name, shape, dt=F32):
            return ctx.enter_context(nc.sbuf_tensor(name, shape, dt))

        xn = sb("xn", [P, STEP, HID])
        xshift = sb("xshift", [P, TILES])
        cos = sb("cos", [P, 2, STEP, P // 2])
        sin = sb("sin", [P, 2, STEP, 2, P // 2])
        win = sb("win", [P, 2, 512], BF16)
        identb = sb("identb", [P, P], BF16)
        cau = sb("cau", [P, 512])
        cum = sb("cum", [P, 130])
        cumh = sb("cumh", [P, 130], F16)
        keep = sb("keep", [P, 2])
        raw_qkv = sb("raw_qkv", [P, QW + KVW])
        raw_o = sb("raw_o", [P, HID])
        wh = sb("wh", [P, 8, WW], F16)
        wl = sb("wl", [P, 8, WW], F16)
        qc = sb("qc", [P, 2, 512])
        qs = sb("qs", [P, 2, 512])
        qe = sb("qe", [P, 2, 512])
        qrT = sb("qrT", [P, 2, 2, GRP, WIN])
        qtT = sb("qtT", [P, 2, GRP, 2, WIN])
        pr = sb("pr", [P, 2, 512])
        am = sb("am", [P, 512])
        pa = sb("pa", [P, 2, 512])
        oT = sb("oT", [P, 2, GRP, 2, WIN], BF16)
        kc = sb("kc", [P, 2, P])
        ks = sb("ks", [P, 2, P])
        kabs = sb("kabs", [P, 2, P])
        kneg = sb("kneg", [P, 2, P])
        gh = sb("gh", [P, 2, P], F16)
        gl = sb("gl", [P, 2, P], F16)
        ke = sb("ke", [P, 2, P])
        ked = sb("ked", [P, 2, P])
        edT = sb("edT", [P, 2, 130])
        kt = sb("kt", [P, 2, P])
        ktT = sb("ktT", [P, 2, P])
        krT = sb("krT", [P, 4, WIN])
        va = sb("va", [P, 4, P])
        vm = sb("vm", [P, 4, P])
        sr = sb("sr", [P, 2, P])
        su = sb("su", [P, P])
        em = sb("em", [P, 2, 1])
        kmx = sb("kmx", [P, 2, 1])
        nkm = sb("nkm", [P, 2, 1])
        ksum = sb("ksum", [P, 2, 1])
        rks = sb("rks", [P, 2, 1])
        qmx = sb("qmx", [P, 2, GRP])
        nqm = sb("nqm", [P, 2, GRP])
        qsum = sb("qsum", [P, 2, GRP])
        rq = sb("rq", [P, 2, GRP])
        pmx = sb("pmx", [P, 2, GRP])
        npm = sb("npm", [P, 2, GRP])
        psm = sb("psm", [P, 2, GRP])
        rp = sb("rp", [P, 2, GRP])
        f_raw = sb("f_raw", [P, NF4_PIECE])
        f_abs = sb("f_abs", [P, NF4_PIECE])
        f_nrm = sb("f_nrm", [P, NF4_PIECE])
        f_max = sb("f_max", [P, 2, NF4_PIECE // BLK])
        f_safe = sb("f_safe", [P, NF4_PIECE // BLK])
        f_rec = sb("f_rec", [P, NF4_PIECE // BLK])
        f_s = sb("f_s", [P, 8, NF4_PIECE])
        f_acc = sb("f_acc", [P, NF4_PIECE])
        f_dq = sb("f_dq", [P, NF4_PIECE])

        PQ, PKV, X0, X1, SC, SM, PO, PW = bank
        names = """q_done kv_done small_done qrT_done at_done sc_done pt_done u_done qsT_done ktT_done o_done
            wo_done v_ev ke_ev e1_ev l1_ev q_exp dec_ev krT_ev qrT_ev p_exp ktT_ev oT_ev
            kmx_d nkm_d kabs_ev kneg_d krope_d g_d gl_d rks_d kt_d qmx_d nqm_d qrope_d rq_d qt_d pmx_d npm_d
            rp_d am_d pa_d su_d em_d sr_d acc_d qrope_p krope_p qn_p pn_p
            wqk_sc wqk_hi wqk_lo wo_sc wo_hi wo_lo raw_a raw_b consts z_id
            x_st x_mv x_var x_sd x_rs x_shift x_norm x_turned x_hi x_lo zeroed id_in
            f_in f_absd f_maxd f_safed f_recd f_nrmd f_sd f_ad f_dqd f_out f_rin f_rest f_rout""".split()
        s = {n: sem("s_" + n) for n in names}
        part_columns = ((0, 256), (256, 512), (512, 768), (QW + KVW, WW))

        def part_of(job, part):
            lo, hi = part_columns[part]
            src = raw_qkv[:, lo:hi] if part < 3 else raw_o[:]
            kind, n = ("wqk", job * 3 + (part + 1)) if part < 3 else ("wo", job + 1)
            return src, lo, hi, s[kind + "_sc"], s[kind + "_hi"], s[kind + "_lo"], n

        x_in = [sem(f"x_in{g}") for g in range(TILES // STEP)]
        x_bank = bank[0:4]
        acc = rows

        t_index = lambda t: t.i % (TILES // STEP)
        block = ctx.enter_context(nc.Block())

        @block.sync
        def _(sp):
            def load_x(g):
                ts = slice(g * STEP, (g + 1) * STEP)
                sp.dma_start(rows[:, ts, :], x_rows[:, ts, :]).then_inc(x_in[g], 16)

            def load_weights(c, k, job):
                if not (isinstance(job, int) and job == 0):
                    sp.wait_ge(s["wqk_lo"], job * 3)
                sp.dma_start(raw_qkv[:, 0:QW], wq_v[c, k]).then_inc(s["raw_a"], 16)
                sp.dma_start(raw_qkv[:, QW:QW + P], wk_v[c, k]).then_inc(s["raw_a"], 16)
                sp.dma_start(raw_qkv[:, QW + P:], wv_v[c, k]).then_inc(s["raw_a"], 16)
                if not (isinstance(job, int) and job == 0):
                    sp.wait_ge(s["wo_lo"], job)
                sp.dma_start(raw_o[:], wo_v[c, k]).then_inc(s["raw_b"], 16)

            def load_piece(i, n):
                if not (isinstance(i, int) and i == 0):
                    sp.wait_ge(s["f_nrmd"], n)
                sp.dma_start(f_raw[:], wf_p[:, i, :]).then_inc(s["f_in"], 16)

            def store_piece(i):
                sp.wait_ge(s["f_dqd"], i + 1)
                sp.dma_start(dq_p[:, i, :], f_dq[:]).then_inc(s["f_out"], 16)

            sp.dma_start(f_dq[:, 0:NF4_REST], wf_v[:, STEPS * NF4_PIECE:]).then_inc(s["f_rin"], 16)
            load_x(0)
            sp.dma_start(ident[:], identc).then_inc(s["id_in"], 16)
            load_x(1)
            load_weights(0, 0, 0)
            for g in range(2, TILES // STEP):
                load_x(g)
            load_weights(1, 0, 1)
            for dst, src in ((cos[:], cosc), (sin[:], sinc), (f_s[:, 0:2, :], winmask), (cau[:], causal), (cum[:], cumsum),
                             (keep[:], keepc)):
                sp.dma_start(dst, src).then_inc(s["consts"], 16)
            for job in range(2, NC):
                load_weights(job, 0, job)
            sp.wait_ge(s["f_rest"], 5 + 29 + 1)
            sp.dma_start(dq_v[:, STEPS * NF4_PIECE:], f_dq[:, 0:NF4_REST]).then_inc(s["f_rout"], 16)
            load_piece(0, 0)
            for c in range(NC):
                load_weights(c, 1, NC + c)
                load_piece(c + 1, c + 1)
                if c:
                    store_piece(c - 1)
            with sp.Fori(1, KVH) as k:
                for c in range(NC):
                    load_weights(c, (k + 1) % KVH, k * NC + (NC + c))
                    load_piece((k * NC + (c + 1)) % STEPS, k * NC + (c + 1))
                    store_piece(k * NC + (c - 1))
            store_piece(STEPS - 1)
            sp.wait_ge(s["f_out"], 16 * STEPS)
            sp.wait_ge(s["f_rout"], 16)

        @block.gpsimd
        def _(pool):
            nc.gpsimd.memset(vm[:], 0.0).then_inc(s["z_id"], 1)

            def rotate_q(t):
                r = t.p % 2
                wait_tile(pool, s["qrope_d"], t)
                nc.gpsimd.tensor_tensor(qc[:, r, :], qc[:, r, :], qs[:, r, :], ALU.add).then_inc(s["qrope_p"], 1)

            def rotate_k(t):
                r = t.p % 2
                wait_tile(pool, s["krope_d"], t)
                nc.gpsimd.tensor_tensor(kc[:, r, :], kc[:, r, :], ks[:, r, :], ALU.add).then_inc(s["krope_p"], 1)

            def softmax_q(t):
                r = t.p % 2
                wait_tile(pool, s["rq_d"], t)
                v = qe[:, r, :].rearrange("p (h n) -> p h n", h=GRP)
                nc.gpsimd.tensor_tensor(v, v, rq[:, r, :].unsqueeze(2).to_broadcast([P, GRP, P]),
                                        ALU.mult).then_inc(s["qn_p"], 1)

            def softmax_p(t):
                r = t.p % 2
                wait_tile(pool, s["rp_d"], t)
                v = pr[:, r, :].rearrange("p (h n) -> p h n", h=GRP)
                nc.gpsimd.tensor_tensor(v, v, rp[:, r, :].unsqueeze(2).to_broadcast([P, GRP, P]),
                                        ALU.mult).then_inc(s["pn_p"], 1)

            def split_low(job, part):
                src, lo, hi, _, high, low, n = part_of(job, part)
                pool.wait_ge(high, n)
                nc.gpsimd.tensor_tensor(wl[:, job % 8, lo:hi], src, wh[:, job % 8, lo:hi], ALU.subtract).then_inc(low, 1)

            def nf4_add(t):
                for k in NF4_STEPS[t.p]:
                    pool.wait_ge(s["f_sd"], t.i * 15 + (k + 1))
                    if k == 1:
                        if not (isinstance(t.i, int) and t.i == 0):
                            pool.wait_ge(s["f_dqd"], t.i)
                        nc.gpsimd.tensor_tensor(f_acc[:], f_s[:, 0, :], f_s[:, 1, :], ALU.add).then_inc(s["f_ad"], 1)
                    elif k > 1:
                        pool.wait_ge(s["f_ad"], t.i * 14 + (k - 1))
                        nc.gpsimd.tensor_tensor(f_acc[:], f_acc[:], f_s[:, k % 8, :], ALU.add).then_inc(s["f_ad"], 1)

            def split_wo(job):
                src, lo, hi, scaled, high, _, n = part_of(job, 3)
                pool.wait_ge(s["raw_b"], (job + 1) * 16)
                nc.gpsimd.tensor_scalar(src, src, WSCALE, None, ALU.mult).then_inc(scaled, 1)
                pool.wait_ge(scaled, n)
                nc.gpsimd.tensor_copy(wh[:, job % 8, lo:hi], src).then_inc(high, 1)
                split_low(job, 3)

            for job in range(NC):
                for part in range(3):
                    split_low(job, part)
                split_wo(job)

            def clear(g):
                nc.gpsimd.memset(acc[:, g * STEP:(g + 1) * STEP, :], 0.0).then_inc(s["zeroed"], 1)

            def turn(t):
                l1 = t.back(1)
                if l1.real():
                    rotate_q(l1)
                if t.real():
                    rotate_k(t)
                if l1.real():
                    softmax_q(l1)
                    nf4_add(l1)
                    softmax_p(l1)
                if t.real():
                    split_low(t.i + NC, t.p)
                if isinstance(t.i, int) and t.i == 0:
                    for g in ((0, 1), (2,), (3,), ())[t.p]:
                        clear(g)

            pool.wait_ge(s["x_norm"], TILES)
            turns(pool, 1, turn)

        @block.scalar
        def _(act):
            def k_exps(t):
                r = t.p % 2
                wait_tile(act, s["kv_done"], t)
                wait_tile(act, s["krope_d"], t)
                wait_tile(act, s["o_done"], t, 3)
                nc.scalar.activation(va[:, t.p, :], PKV[:, P:2 * P], ACT.Copy, scale=0.5 / WSCALE)
                nc.scalar.activation(vm[0:WIN, t.p, :], PKV[0:WIN, P:2 * P], ACT.Copy, scale=0.5 / WSCALE)
                nc.scalar.activation(vm[WIN:P, (t.p + 1) % 4, :], PKV[WIN:P, P:2 * P], ACT.Copy, scale=0.5 / WSCALE)\
                    .then_inc(s["v_ev"], 1)
                wait_tile(act, s["nkm_d"], t)
                nc.scalar.activation(ke[:, r, :], PKV[:, 0:P], ACT.Exp, bias=nkm[:, r, :], scale=1.0 / WSCALE,
                                     accum_out=ksum[:, r, :]).then_inc(s["ke_ev"], 1)
                nc.scalar.activation(kabs[:, r, :], PKV[:, 0:P], ACT.Abs, scale=1.0 / WSCALE).then_inc(s["kabs_ev"], 1)
                wait_tile(act, s["kabs_ev"], t)
                nc.scalar.activation(kabs[:, r, :], kabs[:, r, :], ACT.Exp, scale=-1.0).then_inc(s["e1_ev"], 1)
                wait_tile(act, s["e1_ev"], t)
                nc.scalar.activation(kabs[:, r, :], kabs[:, r, :], ACT.Ln, bias=1.0).then_inc(s["l1_ev"], 1)

            def q_exps(t):
                r = t.p % 2
                wait_tile(act, s["qrope_d"], t)
                wait_tile(act, s["qsT_done"], t, 2)
                for h in range(GRP):
                    last = nc.scalar.activation(qe[:, r, h * P:(h + 1) * P], PQ[:, h * P:(h + 1) * P], ACT.Exp,
                                                bias=nqm[:, r, h:h + 1], scale=1.0 / WSCALE,
                                                accum_out=qsum[:, r, h:h + 1])
                last.then_inc(s["q_exp"], 1)

            def decays(t):
                r = t.p % 2
                wait_tile(act, s["small_done"], t)
                nc.scalar.activation(krT[:, 1 - r, :], SM[:, 260:260 + WIN], ACT.Copy)
                wait_tile(act, s["sc_done"], t, 1)
                nc.scalar.activation(krT[:, 2 + r, :], SM[:, 260 + WIN:260 + P], ACT.Copy).then_inc(s["krT_ev"], 1)
                nc.scalar.activation(ked[:, r, :], SM[:, 0:P], ACT.Exp, scale=-1.0)
                wait_tile(act, s["qt_d"], t, 2)
                wait_tile(act, s["sr_d"], t, 1)
                nc.scalar.activation(edT[:, r, :], SM[:, P:P + 130], ACT.Exp).then_inc(s["dec_ev"], 1)

            def copy_qrT(t):
                wait_tile(act, s["qrT_done"], t)
                wait_tile(act, s["sc_done"], t, 2)
                nc.scalar.activation(qrT[:, t.p % 2].rearrange("p b h n -> p h b n"),
                                     X0[:].rearrange("p (h b n) -> p h b n", h=GRP, b=2), ACT.Copy)\
                    .then_inc(s["qrT_ev"], 1)

            def p_exps(t):
                r = t.p % 2
                wait_tile(act, s["npm_d"], t)
                wait_tile(act, s["pt_done"], t, 2)
                for j in range(GRP):
                    last = nc.scalar.activation(pr[:, r, j * P:(j + 1) * P], SC[:, j * P:(j + 1) * P], ACT.Exp,
                                                bias=npm[:, r, j:j + 1], scale=ATT_SCALE,
                                                accum_out=psm[:, r, j:j + 1])
                last.then_inc(s["p_exp"], 1)

            def copy_ktT(t):
                wait_tile(act, s["ktT_done"], t)
                nc.scalar.activation(ktT[:, t.p % 2, :], SM[:, 0:P], ACT.Copy).then_inc(s["ktT_ev"], 1)

            def nf4_abs(t):
                i = t.i
                if t.p == 0:
                    act.wait_ge(s["f_in"], i * 16 + 16)
                    if isinstance(i, int) and i == 0:
                        act.wait_ge(s["f_rest"], 35)
                    else:
                        act.wait_ge(s["f_maxd"], i)
                    nc.scalar.activation(f_abs[:], f_raw[:], ACT.Abs).then_inc(s["f_absd"], 1)

            def split_high(i, job, part):
                src, lo, hi, scaled, high, _, n = part_of(job, part)
                if part == 0:
                    act.wait_ge(s["raw_a"], (job + 1) * 48)
                if part == 3:
                    act.wait_ge(s["raw_b"], (job + 1) * 16)
                nc.scalar.activation(src, src, ACT.Copy, scale=WSCALE).then_inc(scaled, 1)
                if not (isinstance(i, int) and i <= 0):
                    act.wait_ge(s["q_done"] if part < 3 else s["wo_done"], i * STEP)
                act.wait_ge(scaled, n)
                nc.scalar.activation(wh[:, job % 8, lo:hi], src, ACT.Copy).then_inc(high, 1)

            def copy_o(t):
                wait_tile(act, s["o_done"], t)
                wait_tile(act, s["wo_done"], t, 2)
                nc.scalar.activation(oT[:, t.p % 2].rearrange("p h b n -> p b h n"),
                                     PO[:].rearrange("p (b h n) -> p b h n", b=2, h=GRP), ACT.Copy)\
                    .then_inc(s["oT_ev"], 1)

            def turn(t):
                l1, l3 = t.back(1), t.back(3)
                if l3.real():
                    copy_o(l3)
                if l1.real():
                    q_exps(l1)
                    decays(l1)
                if t.real():
                    k_exps(t)
                    nf4_abs(t)
                if l1.real():
                    copy_qrT(l1)
                    p_exps(l1)
                if t.real():
                    split_high(t.i, t.i + NC, t.p)
                if l1.real():
                    copy_ktT(l1)

            _, _, sd, rs = stats

            def x_deviation(g):
                ts = slice(g * STEP, (g + 1) * STEP)
                act.wait_ge(s["x_var"], g + 1)
                nc.scalar.activation(sd[:, ts], sd[:, ts], ACT.Sqrt).then_inc(s["x_sd"], 1)

            x_deviation(0)
            for g in range(TILES // STEP):
                ts = range(g * STEP, (g + 1) * STEP)
                act.wait_ge(s["x_shift"], g + 1)
                for t in ts:
                    if t >= STEP:
                        act.wait_ge(s["x_turned"], t - STEP + 1)
                    nc.scalar.activation(xn[:, t % STEP, :], rows[:, t, :], ACT.Identity, scale=rs[:, t:t + 1],
                                         bias=xshift[:, t:t + 1]).then_inc(s["x_norm"], 1)
                if g + 1 < TILES // STEP:
                    x_deviation(g + 1)
                for t in ts:
                    act.wait_ge(s["x_turned"], t + 1)
                    nc.scalar.activation(xh[:, :, t, :], x_bank[t % 4][:].rearrange("p (c n) -> p c n", c=NC),
                                         ACT.Copy).then_inc(s["x_hi"], 1)
                for part in range(3):
                    split_high(-1, g, part)
            act.preload_act_table_set("natural_log_exp_and_others")
            turns(act, 3, turn)

        @block.vector
        def _(dve):
            nc.vector.memset(sr[:], 0.0).then_inc(s["sr_d"], 1)
            cos_b = lambda t, n: cos[:, t.i % 2, t.p, :].unsqueeze(1).to_broadcast([P, n, P // 2])
            sin_b = lambda t, half, n: sin[:, t.i % 2, t.p, half, :].unsqueeze(1).to_broadcast([P, n, P // 2])

            def rope(t, src, n, dc, ds, done):
                s4 = src.rearrange("p (h a n) -> p h a n", h=n, a=2)
                d4 = ds.rearrange("p (h a n) -> p h a n", h=n, a=2)
                nc.vector.tensor_tensor(dc.rearrange("p (h n) -> p h n", n=P // 2),
                                        src.rearrange("p (h n) -> p h n", n=P // 2), cos_b(t, 2 * n), ALU.mult)
                nc.vector.tensor_tensor(d4[:, :, 0, :], s4[:, :, 1, :], sin_b(t, 0, n), ALU.mult)
                nc.vector.tensor_tensor(d4[:, :, 1, :], s4[:, :, 0, :], sin_b(t, 1, n), ALU.mult).then_inc(done, 1)

            def use_k(t):
                r = t.p % 2
                wait_tile(dve, s["kv_done"], t)
                nc.vector.tensor_reduce(kmx[:, r, :], PKV[:, 0:P], AX.X, ALU.max).then_inc(s["kmx_d"], 1)
                nc.vector.tensor_scalar(kneg[:, r, :], PKV[:, 0:P], 0.0, 1.0 / WSCALE, ALU.min, ALU.mult)\
                    .then_inc(s["kneg_d"], 1)
                wait_tile(dve, s["kmx_d"], t)
                nc.vector.tensor_scalar(nkm[:, r, :], kmx[:, r, :], -1.0 / WSCALE, None, ALU.mult).then_inc(s["nkm_d"], 1)
                wait_tile(dve, s["small_done"], t, 2)
                rope(t, PKV[:, 0:P], 1, kc[:, r, :], ks[:, r, :], s["krope_d"])

            def log_decay(t):
                r = t.p % 2
                wait_tile(dve, s["l1_ev"], t)
                wait_tile(dve, s["kneg_d"], t)
                wait_tile(dve, s["small_done"], t, 2)
                nc.vector.tensor_tensor(gh[:, r, :], kneg[:, r, :], kabs[:, r, :], ALU.subtract)
                nc.vector.tensor_tensor(kneg[:, r, :], kneg[:, r, :], kabs[:, r, :], ALU.subtract).then_inc(s["g_d"], 1)

            def low_decay(t):
                r = t.p % 2
                wait_tile(dve, s["g_d"], t)
                nc.vector.tensor_tensor(gl[:, r, :], kneg[:, r, :], gh[:, r, :], ALU.subtract).then_inc(s["gl_d"], 1)

            def use_q(t):
                r = t.p % 2
                wait_tile(dve, s["q_done"], t)
                nc.vector.tensor_reduce(qmx[:, r, :], PQ[:].rearrange("p (h n) -> p h n", h=GRP), AX.X, ALU.max)\
                    .then_inc(s["qmx_d"], 1)
                wait_tile(dve, s["qmx_d"], t)
                nc.vector.tensor_scalar(nqm[:, r, :], qmx[:, r, :], -1.0 / WSCALE, None, ALU.mult).then_inc(s["nqm_d"], 1)
                wait_tile(dve, s["qrT_done"], t, 2)
                rope(t, PQ[:], GRP, qc[:, r, :], qs[:, r, :], s["qrope_d"])

            def gla_k(t):
                r = t.p % 2
                wait_tile(dve, s["ke_ev"], t)
                nc.vector.reciprocal(rks[:, r, :], ksum[:, r, :]).then_inc(s["rks_d"], 1)
                wait_tile(dve, s["rks_d"], t)
                wait_tile(dve, s["dec_ev"], t)
                wait_tile(dve, s["u_done"], t, 2)
                nc.vector.scalar_tensor_tensor(out=kt[:, r, :], in0=ke[:, r, :], scalar=rks[:, r, :], in1=ked[:, r, :],
                                               op0=ALU.mult, op1=ALU.mult).then_inc(s["kt_d"], 1)

            def gla_q(t):
                r = t.p % 2
                wait_tile(dve, s["qsT_done"], t)
                wait_tile(dve, s["dec_ev"], t)
                wait_tile(dve, s["o_done"], t, 2)
                nc.vector.tensor_tensor(qtT[:, r].rearrange("p h b n -> p h (b n)"),
                                        X0[:].rearrange("p (h n) -> p h n", h=GRP),
                                        edT[:, r, 0:P].unsqueeze(1).to_broadcast([P, GRP, P]), ALU.mult)\
                    .then_inc(s["qt_d"], 1)

            def q_sums(t):
                r = t.p % 2
                wait_tile(dve, s["q_exp"], t)
                wait_tile(dve, s["qn_p"], t, 2)
                nc.vector.reciprocal(rq[:, r, :], qsum[:, r, :]).then_inc(s["rq_d"], 1)

            def p_max(t):
                r = t.p % 2
                wait_tile(dve, s["sc_done"], t)
                nc.vector.tensor_reduce(pmx[:, r, :], SC[:].rearrange("p (h n) -> p h n", h=GRP), AX.X, ALU.max)\
                    .then_inc(s["pmx_d"], 1)
                wait_tile(dve, s["pmx_d"], t)
                nc.vector.tensor_scalar(npm[:, r, :], pmx[:, r, :], -ATT_SCALE, None, ALU.mult).then_inc(s["npm_d"], 1)

            def p_sums(t):
                r = t.p % 2
                wait_tile(dve, s["p_exp"], t)
                wait_tile(dve, s["pn_p"], t, 2)
                nc.vector.reciprocal(rp[:, r, :], psm[:, r, :]).then_inc(s["rp_d"], 1)

            def mask_gla(t):
                wait_tile(dve, s["at_done"], t)
                wait_tile(dve, s["pa_d"], t, 1)
                nc.vector.tensor_tensor(am[:], X1[:], cau[:], ALU.mult).then_inc(s["am_d"], 1)

            def add_gla(t):
                wait_tile(dve, s["pt_done"], t)
                wait_tile(dve, s["am_d"], t)
                wait_tile(dve, s["o_done"], t, 2)
                nc.vector.tensor_tensor(pa[:, t.p % 2, :], X1[:], am[:], ALU.add).then_inc(s["pa_d"], 1)

            def state(t):
                r, nxt = t.p % 2, t.back(-1)
                wait_tile(dve, s["u_done"], t)
                nc.vector.tensor_tensor(su[:], SM[:, 0:P], sr[:, r, :], ALU.add).then_inc(s["su_d"], 1)
                if not nxt.real():
                    return
                wait_tile(dve, s["dec_ev"], nxt)
                scale = edT[:, 1 - r, P:P + 1]
                if nxt.p == 0:
                    nc.vector.tensor_tensor(em[:, 0, :], scale, keep[:, nxt.i % 2:nxt.i % 2 + 1] if isinstance(nxt.i, int)
                                            else keep[:].unsqueeze(2)[:, nxt.i % 2, :], ALU.mult).then_inc(s["em_d"], 1)
                    dve.wait_ge(s["em_d"], nxt.i)
                    scale = em[:, 0, :]
                wait_tile(dve, s["su_d"], t)
                nc.vector.tensor_scalar(sr[:, 1 - r, :], su[:], edT[:, r, P - 1:P], scale, ALU.mult, ALU.mult)\
                    .then_inc(s["sr_d"], 1)

            def add_out(t):
                if isinstance(t.i, int) and t.i == 0 and t.p == 0:
                    dve.wait_ge(s["zeroed"], TILES // STEP)
                wait_tile(dve, s["wo_done"], t)
                a = acc[:].rearrange("p (g q) n -> p g q n", q=STEP)[:, t_index(t), t.p, :]
                nc.vector.tensor_tensor(a, PW[:], a, ALU.add).then_inc(s["acc_d"], 1)

            def nf4_blocks(i):
                dve.wait_ge(s["f_absd"], i + 1)
                fmax = f_max[:, i % 2, :]
                nc.vector.tensor_reduce(fmax, f_abs[:].rearrange("p (b n) -> p b n", n=BLK), AX.X, ALU.max)\
                    .then_inc(s["f_maxd"], 1)
                dve.wait_ge(s["f_maxd"], i + 1)
                nc.vector.scalar_tensor_tensor(out=f_safe[:], in0=fmax, scalar=0.0, in1=fmax,
                                               op0=ALU.is_equal, op1=ALU.add).then_inc(s["f_safed"], 1)
                dve.wait_ge(s["f_safed"], i + 1)
                nc.vector.reciprocal(f_rec[:], f_safe[:]).then_inc(s["f_recd"], 1)

            def nf4(t):
                i = t.i
                if t.p == 0:
                    dve.wait_ge(s["f_in"], i * 16 + 16)
                    raw3 = f_raw[:].rearrange("p (b n) -> p b n", n=BLK)
                    dve.wait_ge(s["f_recd"], i + 1)
                    nc.vector.tensor_tensor(f_nrm[:].rearrange("p (b n) -> p b n", n=BLK), raw3,
                                            f_rec[:].unsqueeze(2).to_broadcast([P, NF4_PIECE // BLK, BLK]), ALU.mult)\
                        .then_inc(s["f_nrmd"], 1)
                    dve.wait_ge(s["f_nrmd"], i + 1)
                for k in NF4_STEPS[t.p]:
                    if k >= 8:
                        dve.wait_ge(s["f_ad"], i * 14 + max(k - 8, 1))
                    elif not (isinstance(i, int) and i == 0):
                        dve.wait_ge(s["f_ad"], i * 14 - (6 - k if k < 7 else 0))
                    nc.vector.tensor_scalar(f_s[:, k % 8, :], f_nrm[:], float(BOUND[k]), float(DELTA[k]),
                                            ALU.is_gt, ALU.mult).then_inc(s["f_sd"], 1)

            def nf4_end(i):
                dve.wait_ge(s["f_ad"], i * 14 + 14)
                if isinstance(i, int) and i == 0:
                    dve.wait_ge(s["f_rout"], 16)
                else:
                    dve.wait_ge(s["f_out"], i * 16)
                nc.vector.scalar_tensor_tensor(
                    out=f_dq[:].rearrange("p (b n) -> p b n", n=BLK), in0=f_acc[:].rearrange("p (b n) -> p b n", n=BLK),
                    scalar=float(CODE[0]), in1=f_max[:, i % 2, :].unsqueeze(2).to_broadcast([P, NF4_PIECE // BLK, BLK]),
                    op0=ALU.add, op1=ALU.mult).then_inc(s["f_dqd"], 1)

            def turn(t):
                l1, l2, l3 = t.back(1), t.back(2), t.back(3)
                if t.real():
                    use_k(t)
                if l1.real():
                    q_sums(l1)
                if t.p == 1 and not (isinstance(t.i, int) and t.i == 0):
                    nf4_end(t.i - 1)
                if l2.real():
                    mask_gla(l2)
                if l1.real():
                    gla_k(l1)
                if l3.real():
                    add_out(l3)
                if t.real():
                    log_decay(t)
                if l2.real():
                    state(l2)
                    add_gla(l2)
                if l1.real():
                    p_max(l1)
                if t.real():
                    low_decay(t)
                if t.real() and t.p == 0:
                    nf4_blocks(t.i)
                elif t.real():
                    nf4(t)
                if l1.real():
                    p_sums(l1)
                if t.real():
                    use_q(t)
                if l1.real():
                    gla_q(l1)
                if t.real() and t.p == 0:
                    nf4(t)

            def nf4_rest():
                n = NF4_REST
                b = n // BLK
                blocks = lambda a: a[:, 0:n].rearrange("p (b n) -> p b n", n=BLK)
                spread = lambda a: a[:, 0:b].unsqueeze(2).to_broadcast([P, b, BLK])
                done = 0

                def then(ins):
                    nonlocal done
                    done += 1
                    ins.then_inc(s["f_rest"], 1)
                    dve.wait_ge(s["f_rest"], done)

                dve.wait_ge(s["f_rin"], 16)
                then(nc.vector.scalar_tensor_tensor(out=f_abs[:, 0:n], in0=f_dq[:, 0:n], scalar=-1.0, in1=f_dq[:, 0:n],
                                                    op0=ALU.mult, op1=ALU.max))
                then(nc.vector.tensor_reduce(f_max[:, 1, 0:b], blocks(f_abs), AX.X, ALU.max))
                then(nc.vector.scalar_tensor_tensor(out=f_safe[:, 0:b], in0=f_max[:, 1, 0:b], scalar=0.0,
                                                    in1=f_max[:, 1, 0:b], op0=ALU.is_equal, op1=ALU.add))
                then(nc.vector.reciprocal(f_rec[:, 0:b], f_safe[:, 0:b]))
                then(nc.vector.tensor_tensor(blocks(f_nrm), blocks(f_dq), spread(f_rec), ALU.mult))
                then(nc.vector.tensor_scalar(f_acc[:, 0:n], f_nrm[:, 0:n], float(BOUND[0]), float(DELTA[0]),
                                             ALU.is_gt, ALU.mult))
                for k in range(1, 15):
                    then(nc.vector.tensor_scalar(f_abs[:, 0:n], f_nrm[:, 0:n], float(BOUND[k]), float(DELTA[k]),
                                                 ALU.is_gt, ALU.mult))
                    then(nc.vector.tensor_tensor(f_acc[:, 0:n], f_acc[:, 0:n], f_abs[:, 0:n], ALU.add))
                then(nc.vector.scalar_tensor_tensor(out=blocks(f_dq), in0=blocks(f_acc), scalar=float(CODE[0]),
                                                    in1=spread(f_max[:, 1]), op0=ALU.add, op1=ALU.mult))

            def x_statistics(g):
                st, mv, sd, _ = stats
                ts = range(g * STEP, (g + 1) * STEP)
                dve.wait_ge(x_in[g], 16)
                for t in ts:
                    nc.vector.bn_stats(st[:, t, :], rows[:, t, :]).then_inc(s["x_st"], 1)
                for t in ts:
                    dve.wait_ge(s["x_st"], t + 1)
                    nc.vector.bn_aggr(mv[:, t, :], st[:, t, :]).then_inc(s["x_mv"], 1)
                dve.wait_ge(s["x_mv"], (g + 1) * STEP)
                ts = slice(g * STEP, (g + 1) * STEP)
                nc.vector.tensor_scalar(sd[:, ts], mv[:, ts, 1], EPS, None, ALU.add).then_inc(s["x_var"], 1)

            def x_scales(g):
                _, mv, sd, rs = stats
                ts = slice(g * STEP, (g + 1) * STEP)
                dve.wait_ge(s["x_sd"], g + 1)
                nc.vector.reciprocal(rs[:, ts], sd[:, ts]).then_inc(s["x_rs"], 1)
                dve.wait_ge(s["x_rs"], g + 1)
                nc.vector.scalar_tensor_tensor(out=xshift[:, ts], in0=mv[:, ts, 0], scalar=-1.0, in1=rs[:, ts],
                                               op0=ALU.mult, op1=ALU.mult).then_inc(s["x_shift"], 1)

            def x_low(g):
                for t in range(g * STEP, (g + 1) * STEP):
                    dve.wait_ge(s["x_hi"], t + 1)
                    nc.vector.tensor_tensor(xl[:, :, t, :], x_bank[t % 4][:].rearrange("p (c n) -> p c n", c=NC),
                                            xh[:, :, t, :], ALU.subtract).then_inc(s["x_lo"], 1)

            nf4_rest()
            x_statistics(0)
            x_scales(0)
            for g in range(TILES // STEP):
                if g + 1 < TILES // STEP:
                    x_statistics(g + 1)
                    x_scales(g + 1)
                x_low(g)
            dve.wait_ge(s["consts"], 96)
            nc.vector.tensor_copy(identb[:], ident[:]).then_inc(s["z_id"], 1)
            nc.vector.tensor_copy(win[:], f_s[:, 0:2, :]).then_inc(s["z_id"], 1)
            nc.vector.tensor_copy(cumh[:], cum[:]).then_inc(s["z_id"], 1)
            nc.vector.memset(krT[:], 0.0).then_inc(s["z_id"], 1)
            dve.wait_ge(s["z_id"], 5)
            turns(dve, 3, turn)

        @block.tensor
        def _(pe):
            pe.wait_ge(s["id_in"], 16)
            for t in range(TILES):
                pe.wait_ge(s["x_norm"], t + 1)
                if t >= 4:
                    pe.wait_ge(s["x_lo"], t - 3)
                for c in range(NC):
                    last = nc.tensor.transpose(x_bank[t % 4][:, c * P:(c + 1) * P], xn[:, t % STEP, c * P:(c + 1) * P],
                                               ident[:])
                last.then_inc(s["x_turned"], 1)
            pe.wait_ge(s["x_lo"], TILES)
            pe.wait_ge(s["consts"], 96)
            pe.wait_ge(s["z_id"], 5)
            slot = lambda t: (t.i // NC) % 2 * NC

            def decays_and_krT(t):
                r = t.p % 2
                wait_tile(pe, s["gl_d"], t)
                wait_tile(pe, s["krope_p"], t)
                wait_tile(pe, s["ktT_ev"], t, 1)
                for g, start in ((gh, True), (gl, False)):
                    nc.tensor.matmul(SM[:, 0:P], cumh[:, 0:P], g[:, r, :], start=start, stop=not start)
                for g, start in ((gh, True), (gl, False)):
                    nc.tensor.matmul(SM[:, P:P + 130], g[:, r, :], cumh[:], start=start, stop=not start)
                nc.tensor.transpose(SM[:, 260:260 + P], kc[:, r, :], ident[:]).then_inc(s["small_done"], 1)

            def turn_q(t):
                r = t.p % 2
                wait_tile(pe, s["qrope_p"], t)
                wait_tile(pe, s["qt_d"], t, 1)
                for h in range(GRP):
                    last = nc.tensor.transpose(X0[:, h * P:(h + 1) * P], qc[:, r, h * P:(h + 1) * P], ident[:])
                last.then_inc(s["qrT_done"], 1)

            def gla_scores(t):
                r = t.p % 2
                wait_tile(pe, s["qt_d"], t)
                wait_tile(pe, s["ktT_ev"], t)
                wait_tile(pe, s["pa_d"], t, 1)
                nc.tensor.matmul(X1[:], ktT[:, r, :], qtT[:, r].rearrange("p h b n -> p b h n"),
                                 start=True, stop=True).then_inc(s["at_done"], 1)

            def project_out(t):
                if t.p == 0:
                    pe.wait_ge(s["wo_lo"], t.i + NC)
                wait_tile(pe, s["oT_ev"], t)
                wait_tile(pe, s["acc_d"], t, 1)
                sl = slot(t)
                for h in range(GRP):
                    for k, w in enumerate((wh, wl)):
                        last = nc.tensor.matmul(PW[:], oT[:, t.p % 2, h].rearrange("p b n -> p (b n)"),
                                                w[:, sl + h, QW + KVW:WW],
                                                start=(h == 0 and k == 0), stop=(h == GRP - 1 and k == 1))
                last.then_inc(s["wo_done"], 1)

            def project(t, dst, lo, hi, done):
                sl = slot(t)
                n = 0
                for c in range(NC):
                    for a, w in ((xh, wh), (xh, wl), (xl, wh)):
                        av = a[:].rearrange("p c (g q) n -> p c g q n", q=STEP)[:, c, t_index(t), t.p, :]
                        last = nc.tensor.matmul(dst, av, w[:, sl + c, lo:hi], start=(n == 0), stop=(n == 3 * NC - 1))
                        n += 1
                last.then_inc(done, 1)

            def project_q(t):
                wait_tile(pe, s["q_exp"], t, 1)
                project(t, PQ[:], 0, QW, s["q_done"])

            def project_kv(t):
                if t.p == 0:
                    pe.wait_ge(s["wqk_lo"], (t.i + NC) * 3)
                wait_tile(pe, s["kabs_ev"], t, 1)
                project(t, PKV[:, 0:KVW], QW, QW + KVW, s["kv_done"])

            def scores(t):
                r = t.p % 2
                wait_tile(pe, s["krT_ev"], t)
                wait_tile(pe, s["qrT_ev"], t)
                wait_tile(pe, s["p_exp"], t, 1)
                nc.tensor.matmul(SC[:], identb[:], win[:, 1, :] if t.p else win[:, t.i % 2, :], start=True, stop=False)
                low = 1 - r
                for b in range(2):
                    high = 2 + r if b else 3 - r
                    keys = krT[:, low:high + 1:high - low, :]
                    for hp in range(2):
                        j = 2 * b + hp
                        last = nc.tensor.matmul(SC[:, j * P:(j + 1) * P],
                                                qrT[:, r, b, 2 * hp:2 * hp + 2, :].rearrange("p h n -> p (h n)"), keys,
                                                start=False, stop=(j == 3))
                last.then_inc(s["sc_done"], 1)

            def probabilities(t):
                r = t.p % 2
                wait_tile(pe, s["pn_p"], t)
                wait_tile(pe, s["am_d"], t)
                for j in range(GRP):
                    last = nc.tensor.transpose(X1[:, j * P:(j + 1) * P], pr[:, r, j * P:(j + 1) * P], ident[:])
                last.then_inc(s["pt_done"], 1)

            def inter_and_update(t):
                r = t.p % 2
                wait_tile(pe, s["sr_d"], t)
                wait_tile(pe, s["oT_ev"], t, 1)
                nc.tensor.matmul(PO[:], sr[:, r, :], qtT[:, r].rearrange("p h b n -> p b h n"), start=True, stop=False)
                if t.back(-1).real():
                    wait_tile(pe, s["dec_ev"], t.back(-1))
                nc.tensor.matmul(SM[:, 0:P], kt[:, r, :], va[:, t.p, :], start=True, stop=True).then_inc(s["u_done"], 1)

            def qsT_and_ktT(t):
                r = t.p % 2
                wait_tile(pe, s["qn_p"], t)
                wait_tile(pe, s["qrT_ev"], t)
                for h in range(GRP):
                    last = nc.tensor.transpose(X0[:, h * P:(h + 1) * P], qe[:, r, h * P:(h + 1) * P], ident[:])
                last.then_inc(s["qsT_done"], 1)
                wait_tile(pe, s["kt_d"], t)
                wait_tile(pe, s["su_d"], t, 1)
                nc.tensor.transpose(SM[:, 0:P], kt[:, r, :], ident[:]).then_inc(s["ktT_done"], 1)

            def output(t):
                r = t.p % 2
                wait_tile(pe, s["pa_d"], t)
                wait_tile(pe, s["v_ev"], t)
                for b, v in enumerate((vm, va)):
                    last = nc.tensor.matmul(PO[:, b * 256:(b + 1) * 256], v[:, t.p, :], pa[:, r, b * 256:(b + 1) * 256],
                                            start=False, stop=(b == 1))
                last.then_inc(s["o_done"], 1)

            def turn(t):
                l1, l2, l3 = t.back(1), t.back(2), t.back(3)
                if t.real():
                    project_kv(t)
                if l1.real():
                    decays_and_krT(l1)
                if l3.real():
                    project_out(l3)
                if l2.real():
                    gla_scores(l2)
                if l1.real():
                    turn_q(l1)
                if l2.real():
                    inter_and_update(l2)
                    probabilities(l2)
                if l1.real():
                    scores(l1)
                if t.real():
                    project_q(t)
                if l1.real():
                    qsT_and_ktT(l1)
                if l2.real():
                    output(l2)

            turns(pe, 3, turn)


def ffn(nc, sem, bank, rows, xh, xl, ident, stats, x_rows, out_rows, dq):
    with ExitStack() as ctx:
        def sb(name, shape, dt=F32):
            return ctx.enter_context(nc.sbuf_tensor(name, shape, dt))

        w12h = sb("w12h", [P, NC, 2 * FFN], F16)
        w12l = sb("w12l", [P, NC, 2 * FFN], F16)
        w3h = sb("w3h", [P, FC, HID], F16)
        w3l = sb("w3l", [P, FC, HID], F16)
        xr = sb("xr", [P, 2 * STEP, HID])
        xn = sb("xn3", [P, STEP, HID])
        wt = sb("wt", [P, 4, HID])
        norms = {"att": stats, "new": [sb("new_st", [P, TILES, 6]), sb("new_mv", [P, TILES, 2]),
                                       sb("new_sd", [P, TILES]), sb("new_rs", [P, TILES])]}
        shift = {n: sb(n + "_shift", [P, TILES]) for n in norms}
        sg = sb("sg", [P, 2, 512])
        hf = sb("hf", [P, 2, 512])
        hh = sb("hh", [P, 2, 512], F16)
        hl = sb("hl", [P, 2, 512], F16)
        yo = sb("yo", [P, STEP, HID])
        yst = sb("yst", [P, STEP, 6])
        ymv = sb("ymv", [P, STEP, 2])
        ysd = sb("ysd", [P, STEP])
        yrs = sb("yrs", [P, STEP])
        ysh = sb("ysh", [P, STEP])
        r = {n: sem("res_" + n) for n in """att_st att_mv att_var att_sd att_rs att_shift
            new_st new_mv new_var new_sd new_rs new_shift z x1 xn turned high low""".split()}
        x_in = [sem(f"res_in{j}") for j in range(2 * STEP)]
        w_in = [sem(f"wt_in{j}") for j in range(4)]
        f = {n: sem("ffn_" + n) for n in "gate up sg hf hh hl y yq st mv var sd rs shift z za o oa".split()}
        f_out = [sem(f"ffn_out{q}") for q in range(STEP)]
        G, U, turn_bank, Y = bank[0], bank[1], bank[2:4], bank[4:8]
        first_banks = bank[2:8]

        w12_v = dq[0:2 * FFN * HID].rearrange("(r n) -> r n", n=HID)
        w3_v = dq[2 * FFN * HID:].rearrange("(j p n) -> p j n", p=P, n=FFN)
        width = lambda c: P if c < FC - 1 else FLAST
        blocks12 = (2 * FFN + P - 1) // P
        shared = FFN // P
        before = [("w12", j) for j in (0, shared, shared + 1)] + [("x", t) for t in range(STEP)]
        later = TILES // STEP - 1
        TURN_FROM = later + 1
        tiles_of = lambda c: range(STEP + 2 * (c - TURN_FROM), STEP + 2 * (c - TURN_FROM) + 2)
        within = []
        for c in range(FC):
            todo = [("w3", c)]
            if c + 1 < FC:
                todo += [("w12", j) for j in (c + 1, shared + c + 2) if j != shared]
            if c > TURN_FROM:
                todo += [("x", t) for t in tiles_of(c - 1)]
            within.append(todo)
        items = before + [item for todo in within for item in todo]
        place = {item: n for n, item in enumerate(items)}
        jobs = [item for item in items if item[0] != "x"]

        def shown(item):
            kind, j = item
            tb = first_banks[place[item] % 6] if item in before else turn_bank[place[item] % 2]
            if kind == "x":
                src = [xn[:, j % STEP, c * P:(c + 1) * P] for c in range(NC)]
                return src, tb[:].rearrange("p (c n) -> p c n", c=NC), xh[:, :, j, :], xl[:, :, j, :]
            slot = jobs.index(item) % 4
            if kind == "w12":
                m = min(P, 2 * FFN - j * P)
                src = [wt[0:m, slot, c * P:(c + 1) * P] for c in range(NC)]
                return (src, tb[:, 0:NC * m].rearrange("p (c n) -> p c n", c=NC),
                        w12h[:, :, j * P:j * P + m], w12l[:, :, j * P:j * P + m])
            n = width(j)
            src = [wt[:, slot, q * n:(q + 1) * n] for q in range(HID // P)]
            return (src, tb[0:n, :].rearrange("p (c n) -> p c n", n=P),
                    w3h[0:n, j, :].rearrange("p (c n) -> p c n", n=P), w3l[0:n, j, :].rearrange("p (c n) -> p c n", n=P))

        def first(g):
            return isinstance(g, int) and g == 0

        with nc.Block() as block:

            def groups(eng, group):
                group(0)
                with eng.Fori(1, TILES // STEP) as g:
                    group(g)

            def rows_of(g, q):
                return rows[:].rearrange("p (g q) n -> p g q n", q=STEP)[:, g, q, :]

            def after(eng, sm, per, g, n):
                v = g * per + n
                if isinstance(v, int) and v <= 0:
                    return
                eng.wait_ge(sm, v)

            @block.sync
            def _(sp):
                def load_x(t):
                    if t >= 2 * STEP:
                        sp.wait_ge(r["x1"], t - 2 * STEP + 1)
                    sp.dma_start(xr[:, t % (2 * STEP), :], x_rows[:, t, :]).then_inc(x_in[t % (2 * STEP)], 16)

                def load_weights(n):
                    kind, j = jobs[n]
                    if n >= 4:
                        sp.wait_ge(r["turned"], place[jobs[n - 4]] + 1)
                    if kind == "w12":
                        m = min(P, 2 * FFN - j * P)
                        sp.dma_start(wt[0:m, n % 4, :], w12_v[j * P:j * P + m, :]).then_inc(w_in[n % 4], 16)
                    else:
                        m = width(j)
                        sp.dma_start(wt[:, n % 4, 0:m * HID // P].rearrange("p (j n) -> p j n", n=m),
                                     w3_v[:, :, j * P:j * P + m]).then_inc(w_in[n % 4], 16)

                for n in range(3):
                    load_weights(n)
                for t in range(STEP):
                    load_x(t)
                load_weights(3)
                for t in range(STEP, 2 * STEP):
                    load_x(t)
                for n in range(4, len(jobs)):
                    load_weights(n)
                    if n in (5, 8):
                        for t in range(2 * STEP, 3 * STEP) if n == 5 else range(3 * STEP, TILES):
                            load_x(t)

                def group(g):
                    for q in range(STEP):
                        after(sp, f["oa"] if q % 2 else f["o"], STEP // 2, g, q // 2 + 1)
                        out4 = out_rows.rearrange("p (g q) n -> p g q n", q=STEP)
                        sp.dma_start(out4[:, g, q, :], yo[:, q, :]).then_inc(f_out[q], 16)

                groups(sp, group)
                for q in range(STEP):
                    sp.wait_ge(f_out[q], 16 * (TILES // STEP))

            @block.tensor
            def _(pe):
                def turn(item):
                    n = place[item]
                    if item[0] == "x":
                        pe.wait_ge(r["xn"], item[1] + 1)
                    else:
                        k = jobs.index(item)
                        pe.wait_ge(w_in[k % 4], 16 * (k // 4 + 1))
                    ring = 6 if item in before else 2
                    if n >= ring:
                        pe.wait_ge(r["low"], n - ring + 1)
                    src, dst, _, _ = shown(item)
                    for c in range(NC):
                        rows_in = src[c].shape[0]
                        last = nc.tensor.transpose(dst[:, c, :], src[c], ident[0:rows_in, 0:rows_in])
                    last.then_inc(r["turned"], 1)

                def hidden(g, c):
                    n = width(c)
                    todo = within[c] if first(g) else []
                    for dst, off, free, done in ((G, 0, "sg", "gate"), (U, FFN, "hf", "up")):
                        after(pe, f[free], FC, g, c)
                        if first(g) and c == 0 and done == "gate":
                            pe.wait_ge(r["low"], len(before))
                        elif first(g) and done == "gate":
                            pe.wait_ge(r["low"], place[within[c - 1][-1]] + 1)
                        k = 0
                        for d in range(NC):
                            for a, ww in ((xh, w12h), (xl, w12h), (xh, w12l)):
                                x4 = a[:].rearrange("p c (g q) n -> p c g (q n)", q=STEP)[:, d, g, :]
                                last = nc.tensor.matmul(dst[0:n, :], ww[:, d, off + c * P:off + c * P + n], x4,
                                                        start=(k == 0), stop=(k == 3 * NC - 1))
                                k += 1
                            if k == 3 * NC:
                                last.then_inc(f[done], 1)
                            if todo:
                                turn(todo[0])
                                todo = todo[1:]

                def down(g, c):
                    n = width(c)
                    after(pe, f["hl"], FC, g, c + 1)
                    if first(g):
                        pe.wait_ge(r["low"], place[("w3", c)] + 1)
                    if c == 0:
                        after(pe, f["z"], STEP // 2, g, 0)
                        after(pe, f["za"], STEP // 2, g, 0)
                    for q in range(STEP):
                        for k, (a, ww) in enumerate(((hh, w3h), (hh, w3l), (hl, w3h))):
                            last = nc.tensor.matmul(Y[q][:], a[0:n, c % 2, q * P:(q + 1) * P], ww[0:n, c, :],
                                                    start=(c == 0 and k == 0), stop=(c == FC - 1 and k == 2))
                        if c == FC - 1 and q < STEP - 1:
                            last.then_inc(f["yq"], 1)
                    last.then_inc(f["y"], 1)

                def group(g):
                    hidden(g, 0)
                    for c in range(1, FC):
                        hidden(g, c)
                        down(g, c - 1)
                    down(g, FC - 1)

                for item in before:
                    turn(item)
                groups(pe, group)

            @block.scalar
            def _(act):
                def high(item):
                    act.wait_ge(r["turned"], place[item] + 1)
                    _, src, hi, _ = shown(item)
                    nc.scalar.activation(hi, src, ACT.Copy, scale=1.0 if item[0] == "x" else WSCALE)\
                        .then_inc(r["high"], 1)

                def deviation(kind, lo, hi):
                    sd = norms[kind][2][:, lo * STEP:hi * STEP]
                    act.wait_ge(r[kind + "_var"], hi)
                    nc.scalar.activation(sd, sd, ACT.Sqrt).then_inc(r[kind + "_sd"], 1)

                def normalise(kind, tiles):
                    act.wait_ge(r[kind + "_shift"], 2 if tiles[0] >= STEP else 1)
                    for t in tiles:
                        if kind == "new" and t >= STEP:
                            act.wait_ge(r["turned"], place[("x", t - STEP)] + 1)
                        nc.scalar.activation(xn[:, t % STEP, :] if kind == "new" else rows[:, t, :], rows[:, t, :],
                                             ACT.Identity, scale=norms[kind][3][:, t:t + 1],
                                             bias=shift[kind][:, t:t + 1]).then_inc(r["xn" if kind == "new" else "z"], 1)

                def group(g):
                    for c in range(FC):
                        n = width(c)
                        todo = within[c] if first(g) else []
                        for item in todo[0:3]:
                            high(item)
                        after(act, f["gate"], FC, g, c + 1)
                        after(act, f["hf"], FC, g, c - 1)
                        nc.scalar.activation(sg[0:n, c % 2, :], G[0:n, :], ACT.Silu, scale=1.0 / WSCALE)\
                            .then_inc(f["sg"], 1)
                        for item in todo[3:]:
                            high(item)
                        if first(g) and c < later:
                            normalise("att", range((c + 1) * STEP, (c + 2) * STEP))
                        if first(g) and c >= TURN_FROM:
                            if c == TURN_FROM:
                                deviation("new", 1, later + 1)
                            if c < TURN_FROM + 2 * later:
                                normalise("new", tiles_of(c))
                        after(act, f["hf"], FC, g, c + 1)
                        after(act, f["y"], FC, g, c - 1)
                        nc.scalar.activation(hh[0:n, c % 2, :], hf[0:n, c % 2, :], ACT.Copy).then_inc(f["hh"], 1)
                    after(act, f["var"], 1, g, 1)
                    nc.scalar.activation(ysd[:, :], ysd[:, :], ACT.Sqrt).then_inc(f["sd"], 1)
                    after(act, f["shift"], 1, g, 1)
                    for q in range(1, STEP, 2):
                        after(act, f_out[q], 16, g, 0)
                        nc.scalar.activation(yo[:, q, :], Y[q][:], ACT.Identity, scale=yrs[:, q:q + 1],
                                             bias=ysh[:, q:q + 1]).then_inc(f["za"], 1)

                deviation("att", 0, 1)
                normalise("att", range(STEP))
                for item in before[0:3]:
                    high(item)
                deviation("new", 0, 1)
                normalise("new", range(STEP))
                for item in before[3:]:
                    high(item)
                deviation("att", 1, later + 1)
                groups(act, group)

            @block.vector
            def _(dve):
                def low(item):
                    dve.wait_ge(r["high"], place[item] + 1)
                    _, src, hi, lo = shown(item)
                    if item[0] == "x":
                        nc.vector.tensor_tensor(lo, src, hi, ALU.subtract).then_inc(r["low"], 1)
                    else:
                        nc.vector.scalar_tensor_tensor(out=lo, in0=src, scalar=WSCALE, in1=hi,
                                                       op0=ALU.mult, op1=ALU.subtract).then_inc(r["low"], 1)

                def statistics(kind, g):
                    st, mv, sd, _ = norms[kind]
                    ts = range(g * STEP, (g + 1) * STEP)
                    for t in ts:
                        if kind == "new":
                            dve.wait_ge(r["x1"], t + 1)
                        nc.vector.bn_stats(st[:, t, :], rows[:, t, :]).then_inc(r[kind + "_st"], 1)
                    for t in ts:
                        dve.wait_ge(r[kind + "_st"], t + 1)
                        nc.vector.bn_aggr(mv[:, t, :], st[:, t, :]).then_inc(r[kind + "_mv"], 1)
                    dve.wait_ge(r[kind + "_mv"], (g + 1) * STEP)
                    eps = EPS * WSCALE * WSCALE if kind == "att" else EPS
                    nc.vector.tensor_scalar(sd[:, g * STEP:(g + 1) * STEP], mv[:, g * STEP:(g + 1) * STEP, 1], eps, None,
                                            ALU.add).then_inc(r[kind + "_var"], 1)

                def scales(kind, lo, hi):
                    _, mv, sd, rs = norms[kind]
                    ts = slice(lo * STEP, hi * STEP)
                    n = 2 if lo else 1
                    dve.wait_ge(r[kind + "_sd"], n)
                    nc.vector.reciprocal(rs[:, ts], sd[:, ts]).then_inc(r[kind + "_rs"], 1)
                    dve.wait_ge(r[kind + "_rs"], n)
                    nc.vector.scalar_tensor_tensor(out=shift[kind][:, ts], in0=mv[:, ts, 0], scalar=-1.0, in1=rs[:, ts],
                                                   op0=ALU.mult, op1=ALU.mult).then_inc(r[kind + "_shift"], 1)

                def group(g):
                    for c in range(FC):
                        n = width(c)
                        if first(g):
                            for item in within[c]:
                                low(item)
                            if c == TURN_FROM:
                                scales("new", 1, later + 1)
                        after(dve, f["sg"], FC, g, c + 1)
                        after(dve, f["up"], FC, g, c + 1)
                        after(dve, f["hl"], FC, g, c - 1)
                        nc.vector.scalar_tensor_tensor(out=hf[0:n, c % 2, :], in0=U[0:n, :],
                                                       scalar=HSCALE / WSCALE, in1=sg[0:n, c % 2, :],
                                                       op0=ALU.mult, op1=ALU.mult).then_inc(f["hf"], 1)
                        if first(g) and 1 <= c <= later:
                            statistics("new", c)
                    for q in range(STEP):
                        if q < STEP - 1:
                            after(dve, f["yq"], STEP - 1, g, q + 1)
                        else:
                            after(dve, f["y"], FC, g, FC)
                        nc.vector.bn_stats(yst[:, q, :], Y[q][:]).then_inc(f["st"], 1)
                    after(dve, f["st"], STEP, g, STEP)
                    nc.vector.memset(ysd[:, :], 0.0)
                    for q in range(STEP):
                        nc.vector.bn_aggr(ymv[:, q, :], yst[:, q, :]).then_inc(f["mv"], 1)
                    after(dve, f["mv"], STEP, g, STEP)
                    nc.vector.tensor_scalar(ysd[:, :], ymv[:, :, 1], EPS * (WSCALE * HSCALE) ** 2, None, ALU.add)\
                        .then_inc(f["var"], 1)
                    after(dve, f["sd"], 1, g, 1)
                    after(dve, f["za"], STEP // 2, g, 0)
                    nc.vector.reciprocal(yrs[:, :], ysd[:, :]).then_inc(f["rs"], 1)
                    after(dve, f["rs"], 1, g, 1)
                    nc.vector.scalar_tensor_tensor(out=ysh[:, :], in0=ymv[:, :, 0], scalar=-1.0, in1=yrs[:, :],
                                                   op0=ALU.mult, op1=ALU.mult).then_inc(f["shift"], 1)
                    for q in range(0, STEP, 2):
                        after(dve, f_out[q], 16, g, 0)
                        nc.vector.tensor_scalar(yo[:, q, :], Y[q][:], ymv[:, q, 0:1], yrs[:, q:q + 1],
                                                ALU.subtract, ALU.mult).then_inc(f["z"], 1)
                    for n, q in enumerate(range(0, STEP, 2)):
                        after(dve, f["z"], STEP // 2, g, n + 1)
                        nc.vector.tensor_tensor(yo[:, q, :], yo[:, q, :], rows_of(g, q), ALU.add).then_inc(f["o"], 1)

                statistics("att", 0)
                scales("att", 0, 1)
                statistics("att", 1)
                for item in before[0:3]:
                    low(item)
                statistics("new", 0)
                scales("new", 0, 1)
                for item in before[3:]:
                    low(item)
                for g in range(2, later + 1):
                    statistics("att", g)
                scales("att", 1, later + 1)
                groups(dve, group)

            @block.gpsimd
            def _(pool):
                def residual(g):
                    for t in range(g * STEP, (g + 1) * STEP):
                        pool.wait_ge(x_in[t % (2 * STEP)], 16 * (t // (2 * STEP) + 1))
                        pool.wait_ge(r["z"], t + 1)
                        nc.gpsimd.tensor_tensor(rows[:, t, :], rows[:, t, :], xr[:, t % (2 * STEP), :], ALU.add)\
                            .then_inc(r["x1"], 1)

                def group(g):
                    for c in range(FC):
                        n = width(c)
                        after(pool, f["hh"], FC, g, c + 1)
                        after(pool, f["y"], FC, g, c - 1)
                        nc.gpsimd.tensor_tensor(hl[0:n, c % 2, :], hf[0:n, c % 2, :], hh[0:n, c % 2, :], ALU.subtract)\
                            .then_inc(f["hl"], 1)
                        if first(g) and c < later:
                            residual(c + 1)
                    for n, q in enumerate(range(1, STEP, 2)):
                        after(pool, f["za"], STEP // 2, g, n + 1)
                        nc.gpsimd.tensor_tensor(yo[:, q, :], yo[:, q, :], rows_of(g, q), ALU.add).then_inc(f["oa"], 1)

                residual(0)
                groups(pool, group)


def constants():
    half = np.arange(P // 2, dtype=np.float32)
    inv = (np.float32(1.0) / np.power(np.float32(10000.0), np.float32(2.0) * half / np.float32(P))).astype(np.float32)
    fr = np.arange(SEQ, dtype=np.float32)[:, None] * inv[None, :]
    lay = lambda a: np.ascontiguousarray(a.reshape(TPB, P, P // 2).transpose(1, 0, 2).reshape(P, 2, STEP, P // 2))
    cos = lay(np.cos(fr).astype(np.float32) / np.float32(WSCALE))
    sn = lay(np.sin(fr).astype(np.float32) / np.float32(WSCALE))
    sin = np.ascontiguousarray(np.stack([-sn, sn], axis=3))
    a = np.arange(P)[:, None] % WIN
    slot = np.arange(P)[None, :]
    win = np.zeros((P, 2, 2, 2, P), np.float32)
    c0 = np.where(slot < WIN, slot + WIN, slot - WIN)
    c1 = slot
    for ver in range(2):
        for b, c in enumerate((c0, c1)):
            ok = (a + WIN - c >= 0) & (a + WIN - c <= WIN)
            if ver == 0 and b == 0:
                ok = ok & (c >= WIN)
            win[:, ver, b, :, :] = np.where(ok, 0.0, MASKED)[:, None, :]
    win = np.ascontiguousarray(win.reshape(P, 2, 512))
    j = np.arange(P)[:, None]
    i = np.arange(P)[None, :]
    cau = (j <= i).astype(np.float32).reshape(P, 2, 1, WIN)
    cau = np.ascontiguousarray(np.broadcast_to(cau, (P, 2, GRP, WIN)).reshape(P, 512))
    mid = P // 2 - 1
    cum = np.zeros((P, 130), np.float32)
    cum[:, 0:P] = ((j > mid) & (j <= i)).astype(np.float32) - ((j <= mid) & (j > i)).astype(np.float32)
    cum[:, P] = (np.arange(P) <= mid)
    cum /= 16.0
    keep = np.ones((P, 2), np.float32)
    keep[:, 0] = 0.0
    return {"cosc": cos, "sinc": sin, "winmask": win, "causal": cau, "cumsum": cum,
            "identc": np.eye(P, dtype=np.float32), "keepc": keep}


def kernel(L0_attn_hidden_states, L0_attn_Wq, L0_attn_Wk, L0_attn_Wv, L0_attn_Wo, L0_ffn_w1, L0_ffn_w2, L0_ffn_w3):
    import concourse.bacc as _bacc
    from concourse.bass_utils import run_bass_kernel_spmd as _run

    nc = _bacc.Bacc("TRN2", target_bir_lowering=False, num_devices=1)
    arrays = {
        "x": L0_attn_hidden_states, "wq": L0_attn_Wq, "wk": L0_attn_Wk, "wv": L0_attn_Wv, "wo": L0_attn_Wo,
        "wf": np.concatenate([np.asarray(w).reshape(-1) for w in (L0_ffn_w1, L0_ffn_w2, L0_ffn_w3)]),
    }
    arrays = {k: np.ascontiguousarray(v) for k, v in arrays.items()}
    arrays.update(constants())
    args = [nc.dram_tensor(k, v.shape, mybir.dt.from_np(v.dtype), kind="ExternalInput").ap() for k, v in arrays.items()]
    dq = nc.dram_tensor("dequantised", (3 * FFN * HID,), F32, kind="Internal").ap()
    out = nc.dram_tensor("out", (BATCH, SEQ, HID), F32, kind="ExternalOutput").ap()
    layer(nc, *args, dq, out)
    return _run(nc, [arrays], core_ids=[0]).results[0]["out"]
```
